# Optimizing a Trainium2 kernel written in Bass

```python
import numpy as np
import jax
import jax.numpy as jnp

def _softmax(x, axis=-1):
    return jax.nn.softmax(x, axis=axis)

def _gelu(x):
    return jax.nn.gelu(x, approximate=True)

def _silu(x):
    return jax.nn.silu(x)

def _sigmoid(x):
    return jax.nn.sigmoid(x)

def _layernorm(x, axis=-1, eps=1e-05):
    m = jnp.mean(x, axis=axis, keepdims=True)
    v = jnp.var(x, axis=axis, keepdims=True)
    return (x - m) / jnp.sqrt(v + eps)

def _scatter_add(tgt, idx, src, axis=0):
    return tgt.at[idx].add(src)

def _segment_sum(src, seg, n):
    return jax.ops.segment_sum(src, seg, n)
kernel_name = 'mk_recurrent_d1_jaxref_r8_6d16ad'

def setup_inputs(seed: int=0):
    np.random.seed(seed)
    _w = jnp.asarray

    def _L0_attn_setup():
        import jax, jax.numpy as jnp
        import numpy as np
        B, S, D = (4, 256, 128)
        H = 16
        HD = D // H
        key = jax.random.key(seed)
        ks = jax.random.split(key, 6)
        scale = 1.0 / np.sqrt(D)
        x = jax.random.normal(ks[0], (B, S, D), dtype=jnp.float32)
        Wq = jax.random.normal(ks[1], (D, D), dtype=jnp.float32) * scale
        Wk = jax.random.normal(ks[2], (D, D), dtype=jnp.float32) * scale
        Wv = jax.random.normal(ks[3], (D, D), dtype=jnp.float32) * scale
        Wo = jax.random.normal(ks[4], (D, D), dtype=jnp.float32) * scale
        bo = jax.random.normal(ks[5], (D,), dtype=jnp.float32) * 0.01
        return {'x': x, 'Wq': Wq, 'Wk': Wk, 'Wv': Wv, 'Wo': Wo, 'bo': bo}
    _L0_attn_in = _L0_attn_setup()

    def _L0_ffn_setup():
        import jax, jax.numpy as jnp
        import numpy as np
        DIM = 128
        DEPTH = 6
        HEADS = 16
        DIM_HEAD = 64
        WINDOW = 32
        INNER = HEADS * DIM_HEAD
        DIM_INNER = int(DIM * 4 * 2 / 3)
        QK_SCALE = 8.0

        def shift_tokens(t):
            a, s = jnp.split(t, 2, -1)
            s = jnp.pad(s, ((0, 0), (1, 0), (0, 0)))[:, :-1]
            return jnp.concatenate([a, s], -1)

        def l2norm(t):
            return t / jnp.maximum(jnp.linalg.norm(t, axis=-1, keepdims=True), 1e-12)

        def rotate_half(x):
            x1, x2 = jnp.split(x, 2, -1)
            return jnp.concatenate([-x2, x1], -1)

        def rotary_tables(n):
            half = jnp.arange(0, DIM_HEAD, 2, dtype=jnp.float32)
            inv_freq = 1.0 / 10000.0 ** (half / DIM_HEAD)
            t = jnp.arange(n, dtype=jnp.float32)
            freqs = t[:, None] * inv_freq[None, :]
            freqs = jnp.concatenate([freqs, freqs], -1)
            base_scale = (half + 0.4 * DIM_HEAD) / (1.4 * DIM_HEAD)
            power = (t - n // 2) / (WINDOW // 2)
            scale = base_scale[None, :] ** power[:, None]
            scale = jnp.concatenate([scale, scale], -1)
            return (freqs, scale)

        def local_attention(q, k, v):
            b, h, n, d = q.shape
            w = WINDOW
            nw = n // w
            bq = q.reshape(b, h, nw, w, d)
            bk = k.reshape(b, h, nw, w, d)
            bv = v.reshape(b, h, nw, w, d)

            def look(t):
                p = jnp.pad(t, ((0, 0), (0, 0), (1, 0), (0, 0), (0, 0)))
                return jnp.concatenate([p[:, :, :nw], p[:, :, 1:]], axis=3)
            bk2, bv2 = (look(bk), look(bv))
            seq = jnp.arange(n).reshape(nw, w)
            seq_p = jnp.pad(seq, ((1, 0), (0, 0)), constant_values=-1)
            jt = jnp.concatenate([seq_p[:nw], seq_p[1:]], axis=1)
            it = seq[:, :, None]
            jb = jt[:, None, :]
            mask = (it < jb) | (it > jb + w) | (jb == -1)
            sim = jnp.einsum('bhwie,bhwje->bhwij', bq, bk2) * QK_SCALE
            sim = jnp.where(mask, -jnp.finfo(sim.dtype).max, sim)
            attn = jax.nn.softmax(sim, -1)
            out = jnp.einsum('bhwij,bhwje->bhwie', attn, bv2)
            return out.reshape(b, h, n, d)

        def attn_layer(x, Wqkv, qs, ksc, Wo):
            b, n, _ = x.shape
            qkv = x @ Wqkv
            q, k, v = jnp.split(qkv, 3, -1)
            sh = lambda t: t.reshape(b, n, HEADS, DIM_HEAD).transpose(0, 2, 1, 3)
            q, k, v = (sh(q), sh(k), sh(v))
            q = l2norm(q) * qs
            k = l2norm(k) * ksc
            freqs, scale = rotary_tables(n)
            cos, sin = (jnp.cos(freqs), jnp.sin(freqs))
            q = q * cos * scale + rotate_half(q) * sin * scale
            inv = 1.0 / scale
            k = k * cos * inv + rotate_half(k) * sin * inv
            out = local_attention(q, k, v)
            out = out.transpose(0, 2, 1, 3).reshape(b, n, INNER)
            return out @ Wo

        def ffn_layer(x, g, bln, W1, b1, W2, b2):
            mu = x.mean(-1, keepdims=True)
            var = ((x - mu) ** 2).mean(-1, keepdims=True)
            xn = (x - mu) / jnp.sqrt(var + 1e-05) * g + bln
            hg = xn @ W1 + b1
            a, gate = jnp.split(hg, 2, -1)
            return a * jax.nn.gelu(gate, approximate=False) @ W2 + b2
        key = jax.random.key(seed)
        ks = jax.random.split(key, 8)
        B, N = (2, 256)
        init = lambda k, shape: jax.random.normal(k, shape, jnp.float32) * 0.02
        return {'x': jax.random.normal(ks[0], (B, N, DIM), jnp.float32), 'Wqkv': init(ks[1], (DEPTH, DIM, 3 * INNER)), 'q_scale': jnp.ones((DEPTH, DIM_HEAD), jnp.float32), 'k_scale': jnp.ones((DEPTH, DIM_HEAD), jnp.float32), 'Wo': init(ks[2], (DEPTH, INNER, DIM)), 'ln_g': jnp.ones((DEPTH, DIM), jnp.float32), 'ln_b': jnp.zeros((DEPTH, DIM), jnp.float32), 'W1': init(ks[3], (DEPTH, DIM, 2 * DIM_INNER)), 'b1': jnp.zeros((DEPTH, 2 * DIM_INNER), jnp.float32), 'W2': init(ks[4], (DEPTH, DIM_INNER, DIM)), 'b2': jnp.zeros((DEPTH, DIM), jnp.float32)}
    _L0_ffn_in = _L0_ffn_setup()
    _d = {'L0_attn_x': _L0_attn_in['x'], 'L0_attn_Wq': _L0_attn_in['Wq'], 'L0_attn_Wk': _L0_attn_in['Wk'], 'L0_attn_Wv': _L0_attn_in['Wv'], 'L0_attn_Wo': _L0_attn_in['Wo'], 'L0_attn_bo': _L0_attn_in['bo'], 'L0_ffn_Wqkv': _L0_ffn_in['Wqkv'], 'L0_ffn_q_scale': _L0_ffn_in['q_scale'], 'L0_ffn_k_scale': _L0_ffn_in['k_scale'], 'L0_ffn_Wo': _L0_ffn_in['Wo'], 'L0_ffn_ln_g': _L0_ffn_in['ln_g'], 'L0_ffn_ln_b': _L0_ffn_in['ln_b'], 'L0_ffn_W1': _L0_ffn_in['W1'], 'L0_ffn_b1': _L0_ffn_in['b1'], 'L0_ffn_W2': _L0_ffn_in['W2'], 'L0_ffn_b2': _L0_ffn_in['b2']}
    _x0 = _d['L0_attn_x']
    _d['L0_attn_x'] = jax.random.normal(jax.random.fold_in(jax.random.key(seed), 1), (8, 512, 128), dtype=_x0.dtype)
    del _x0
    return _d

def reference(L0_attn_x, L0_attn_Wq, L0_attn_Wk, L0_attn_Wv, L0_attn_Wo, L0_attn_bo, L0_ffn_Wqkv, L0_ffn_q_scale, L0_ffn_k_scale, L0_ffn_Wo, L0_ffn_ln_g, L0_ffn_ln_b, L0_ffn_W1, L0_ffn_b1, L0_ffn_W2, L0_ffn_b2):

    def _L0_attn_ref(x, Wq, Wk, Wv, Wo, bo):
        import jax, jax.numpy as jnp
        import numpy as np
        B, S, D = (4, 256, 128)
        H = 16
        HD = D // H
        b, n, _ = x.shape
        q = (x @ Wq).reshape(b, n, H, HD).transpose(0, 2, 1, 3)
        k = (x @ Wk).reshape(b, n, H, HD).transpose(0, 2, 1, 3)
        v = (x @ Wv).reshape(b, n, H, HD).transpose(0, 2, 1, 3)
        scores = jnp.einsum('bhqd,bhkd->bhqk', q, k) / jnp.sqrt(jnp.float32(HD))
        causal = jnp.tril(jnp.ones((n, n), dtype=bool))
        scores = jnp.where(causal, scores, -jnp.inf)
        attn = jax.nn.softmax(scores, axis=-1)
        ctx = jnp.einsum('bhqk,bhkd->bhqd', attn, v)
        ctx = ctx.transpose(0, 2, 1, 3).reshape(b, n, D)
        return ctx @ Wo + bo

    def _L0_ffn_ref(x, Wqkv, q_scale, k_scale, Wo, ln_g, ln_b, W1, b1, W2, b2):
        import jax, jax.numpy as jnp
        import numpy as np
        DIM = 128
        DEPTH = 6
        HEADS = 16
        DIM_HEAD = 64
        WINDOW = 32
        INNER = HEADS * DIM_HEAD
        DIM_INNER = int(DIM * 4 * 2 / 3)
        QK_SCALE = 8.0

        def shift_tokens(t):
            a, s = jnp.split(t, 2, -1)
            s = jnp.pad(s, ((0, 0), (1, 0), (0, 0)))[:, :-1]
            return jnp.concatenate([a, s], -1)

        def l2norm(t):
            return t / jnp.maximum(jnp.linalg.norm(t, axis=-1, keepdims=True), 1e-12)

        def rotate_half(x):
            x1, x2 = jnp.split(x, 2, -1)
            return jnp.concatenate([-x2, x1], -1)

        def rotary_tables(n):
            half = jnp.arange(0, DIM_HEAD, 2, dtype=jnp.float32)
            inv_freq = 1.0 / 10000.0 ** (half / DIM_HEAD)
            t = jnp.arange(n, dtype=jnp.float32)
            freqs = t[:, None] * inv_freq[None, :]
            freqs = jnp.concatenate([freqs, freqs], -1)
            base_scale = (half + 0.4 * DIM_HEAD) / (1.4 * DIM_HEAD)
            power = (t - n // 2) / (WINDOW // 2)
            scale = base_scale[None, :] ** power[:, None]
            scale = jnp.concatenate([scale, scale], -1)
            return (freqs, scale)

        def local_attention(q, k, v):
            b, h, n, d = q.shape
            w = WINDOW
            nw = n // w
            bq = q.reshape(b, h, nw, w, d)
            bk = k.reshape(b, h, nw, w, d)
            bv = v.reshape(b, h, nw, w, d)

            def look(t):
                p = jnp.pad(t, ((0, 0), (0, 0), (1, 0), (0, 0), (0, 0)))
                return jnp.concatenate([p[:, :, :nw], p[:, :, 1:]], axis=3)
            bk2, bv2 = (look(bk), look(bv))
            seq = jnp.arange(n).reshape(nw, w)
            seq_p = jnp.pad(seq, ((1, 0), (0, 0)), constant_values=-1)
            jt = jnp.concatenate([seq_p[:nw], seq_p[1:]], axis=1)
            it = seq[:, :, None]
            jb = jt[:, None, :]
            mask = (it < jb) | (it > jb + w) | (jb == -1)
            sim = jnp.einsum('bhwie,bhwje->bhwij', bq, bk2) * QK_SCALE
            sim = jnp.where(mask, -jnp.finfo(sim.dtype).max, sim)
            attn = jax.nn.softmax(sim, -1)
            out = jnp.einsum('bhwij,bhwje->bhwie', attn, bv2)
            return out.reshape(b, h, n, d)

        def attn_layer(x, Wqkv, qs, ksc, Wo):
            b, n, _ = x.shape
            qkv = x @ Wqkv
            q, k, v = jnp.split(qkv, 3, -1)
            sh = lambda t: t.reshape(b, n, HEADS, DIM_HEAD).transpose(0, 2, 1, 3)
            q, k, v = (sh(q), sh(k), sh(v))
            q = l2norm(q) * qs
            k = l2norm(k) * ksc
            freqs, scale = rotary_tables(n)
            cos, sin = (jnp.cos(freqs), jnp.sin(freqs))
            q = q * cos * scale + rotate_half(q) * sin * scale
            inv = 1.0 / scale
            k = k * cos * inv + rotate_half(k) * sin * inv
            out = local_attention(q, k, v)
            out = out.transpose(0, 2, 1, 3).reshape(b, n, INNER)
            return out @ Wo

        def ffn_layer(x, g, bln, W1, b1, W2, b2):
            mu = x.mean(-1, keepdims=True)
            var = ((x - mu) ** 2).mean(-1, keepdims=True)
            xn = (x - mu) / jnp.sqrt(var + 1e-05) * g + bln
            hg = xn @ W1 + b1
            a, gate = jnp.split(hg, 2, -1)
            return a * jax.nn.gelu(gate, approximate=False) @ W2 + b2
        for i in range(DEPTH):
            x = attn_layer(shift_tokens(x), Wqkv[i], q_scale[i], k_scale[i], Wo[i]) + x
            x = ffn_layer(shift_tokens(x), ln_g[i], ln_b[i], W1[i], b1[i], W2[i], b2[i]) + x
        return x
    x = L0_attn_x
    xn = _layernorm(x, axis=-1)
    s = _L0_attn_ref(xn, L0_attn_Wq, L0_attn_Wk, L0_attn_Wv, L0_attn_Wo, L0_attn_bo)
    g = _silu(_L0_ffn_ref(xn, L0_ffn_Wqkv, L0_ffn_q_scale, L0_ffn_k_scale, L0_ffn_Wo, L0_ffn_ln_g, L0_ffn_ln_b, L0_ffn_W1, L0_ffn_b1, L0_ffn_W2, L0_ffn_b2))
    x = x + s * g
    return x

_drawn_inputs = setup_inputs


def setup_inputs(seed=0):
    import zlib

    import numpy as np

    out = dict(_drawn_inputs(seed))
    spreads = {'L0_ffn_q_scale': (1.0, 0.6),
     'L0_ffn_k_scale': (1.0, 0.6),
     'L0_ffn_ln_g': (1.0, 0.6),
     'L0_ffn_ln_b': (0.0, 0.8),
     'L0_ffn_b1': (0.0, 0.8),
     'L0_ffn_b2': (0.0, 0.279)}
    factors = {'L0_attn_bo': 7.474,
     'L0_ffn_Wqkv': 3.597,
     'L0_ffn_Wo': 3.604,
     'L0_ffn_W1': 8.0,
     'L0_ffn_W2': 8.0}
    for name, (base, spread) in spreads.items():
        noise = np.random.default_rng([zlib.crc32(name.encode()), seed]).standard_normal(out[name].shape)
        drawn = base * np.exp(spread * noise) if base else spread * noise
        out[name] = jnp.asarray(drawn.astype(out[name].dtype))
    for name, factor in factors.items():
        out[name] = (out[name] * factor).astype(out[name].dtype)
    return out
```

```python
import numpy as np
import concourse.bass as bass
from concourse import mybir
from contextlib import ExitStack

NSEQ, S, D = 8, 512, 128
TT = S // 128
DEPTH = 6
H = 16
CH = D // H
DH, INNER = 64, 16 * 64
PAIRS = H // 2
W = 32
QT = 96
NT = -(-S // QT)
FF = int(D * 4 * 2 / 3)
FC = -(-FF // 3)
CHUNK = [min(FC, FF - FC * j) for j in range(3)]
EPS = 1e-5
NEG = -1.0e30
WCOLS = 3 * INNER + PAIRS * D
FCOLS = 2 * FF + 3 * D + 3 + 6

UNITS = NT * 4
QKJOBS = 2 * TT
PROJ_SLOT = [11 + 3 * j for j in range(QKJOBS)]
TURN_SLOT = [13 + 3 * j for j in range(QKJOBS)]
V_SLOT = [12 + 3 * v for v in range(NT)]
JOBS = sorted([(s, 0, "proj", j) for j, s in enumerate(PROJ_SLOT)]
              + [(s, 0, "turn", j) for j, s in enumerate(TURN_SLOT)]
              + [(s, 0, "v", v) for v, s in enumerate(V_SLOT)])


def tile_queries(t):
    return min(QT, S - QT * t)


def tile_keys(t):
    return min(128, S - QT * t + W)


def jobs_at(slot, own, following):
    out = []
    if own:
        out += [(k, j, 0) for s, _, k, j in JOBS if s == slot + UNITS]
    if following and slot < UNITS:
        out += [(k, j, 1) for s, _, k, j in JOBS if s == slot]
    return out


def before(kind, j):
    i = [(k, n) for _, _, k, n in JOBS].index((kind, j))
    s = JOBS[i][0]
    order = sorted([((a % UNITS), k, n, a // UNITS) for a, _, k, n in JOBS])
    at = [(k, n) for _, k, n, _ in order].index((kind, j))
    k, n = order[at - 1][1:3]
    wraps = 1 if at == 0 else 0
    return k, n, order[at - 1][3] - s // UNITS + wraps


NEWTON = 3
RSQRT_STEPS = 2 + 3 * NEWTON
MAGIC = float(0x5f3759df)


class Tally:

    def __init__(self, sem, per_seq, head_start=0):
        self.sem, self.per_seq, self.head_start = sem, per_seq, head_start

    def at(self, layer, seq, n):
        return layer * (NSEQ * self.per_seq) + seq * self.per_seq + (n + 1 + self.head_start)


def build(nc, x_in, table_in, qkscale_in, ident_in, mask_in, wqk1_in, wvo1_in, bo_in, wattn_in, wffn_in, out):
    fp32, bf16 = mybir.dt.float32, mybir.dt.bfloat16
    ALU, ACT, AX = mybir.AluOpType, mybir.ActivationFunctionType, mybir.AxisListType
    ds = bass.ds

    with ExitStack() as ctx:
        def sb(name, shape, dt=fp32):
            return ctx.enter_context(nc.sbuf_tensor(name, shape, dt))

        def sem(name):
            return ctx.enter_context(nc.semaphore(name))

        def tally(name, per_seq, head_start=0):
            return Tally(sem(name), per_seq, head_start)

        x = sb("x", [128, NSEQ * S])
        sa = sb("sa", [128, NSEQ * S])
        wattn = sb("wattn", [128, WCOLS])
        wffn = sb("wffn", [128, FCOLS])
        wqk1 = sb("wqk1", [128, 8, 128])
        wvo1 = sb("wvo1", [128, 2, 128])
        bo = sb("bo", [128, 1])
        ident = sb("ident", [128, 128])
        ident_b = sb("ident_b", [128, 128], bf16)
        maskf = sb("maskf", [128, 3, 128])
        mask = sb("mask", [128, 3, 128], bf16)
        table = sb("table", [128, 4, TT, DH])
        qkscale = sb("qkscale", [128, DEPTH * 4 * DH])
        ltable = sb("ltable", [128, 4, TT, DH])
        mean_w = sb("mean_w", [128, 128])
        xs = sb("xs", [128, W + S])
        qT = sb("qT", [128, PAIRS, S])
        kT = sb("kT", [128, PAIRS, W + S])
        v = sb("v", [128, NT, INNER])
        oT = sb("oT", [128, PAIRS, S])
        sq = sb("sq", [128, H * DH])
        rot = sb("rot", [128, H * DH])
        rot_s = sb("rot_s", [128, H * DH])
        n2 = sb("n2", [128, H])
        rn = sb("rn", [128, 2, H])
        rtmp = sb("rtmp", [128, 2, H])
        p = sb("p", [128, 2, 512])
        pT = sb("pT", [128, 2, 512])
        nmax = sb("nmax", [128, 2, 4])
        psums = sb("psums", [128, 2, H])
        rinv = sb("rinv", [128, 2, H])
        osb = sb("osb", [128, 2, 512])
        xm = sb("xm", [128, S])
        xc = sb("xc", [128, S])
        xc2 = sb("xc2", [128, S])
        rstd = sb("rstd", [128, 3, TT])
        diag = sb("diag", [128, S])
        ones = sb("ones", [128, 128])
        xd = sb("xd", [128, S])
        xn = sb("xn", [128, S])
        gate = sb("gate", [128, 3, S])
        hid = sb("hid", [128, 3, S])
        st = sb("st", [128, 6, TT])

        xtok = v[:, :, :].rearrange("p a b -> p (a b)")[:, 0:NSEQ * S]
        qT1 = qT[:, 0:4, :]
        kT1 = qT[:, 4:8, :]
        v1 = oT[:, 0, :].rearrange("p (t c) -> p t c", t=TT)
        oT1 = oT[:, 1, :]
        xb = oT[:, 2, :]
        xtn = oT[:, 3, :].rearrange("p (t c) -> p t c", t=TT)
        xtc = oT[:, 4, :].rearrange("p (t c) -> p t c", t=TT)
        xtq = oT[:, 5, :].rearrange("p (t c) -> p t c", t=TT)

        pj = ctx.enter_context(nc.psum_tensor("pj", [128, 2, 512], fp32))
        sc = ctx.enter_context(nc.psum_tensor("sc", [128, 2, 512], fp32))
        tp = ctx.enter_context(nc.psum_tensor("tp", [128, 2, 512], fp32))
        ob = ctx.enter_context(nc.psum_tensor("ob", [128, 2, 512], fp32))

        const_in, table_in_s, x_loaded, xtok_loaded, stored = sem("const_in"), sem("table_loaded"), sem("x_loaded"), sem("xtok_loaded"), sem("stored")
        wattn_in_s, wffn_in_s = sem("wattn_loaded"), sem("wffn_loaded")
        waits_past = sem("waits_past")
        const_ready, zero_ready = sem("const_ready"), sem("zero_ready")
        F = 4 * H
        f_ln = tally("f_ln", 6 + RSQRT_STEPS)
        f_xn = tally("f_xn", 1)
        f_xt = tally("f_xt", 1)
        f_x = tally("f_x", 1)
        f_pj = tally("f_pj", 9)
        f_pe = tally("f_pe", 9, 2)
        f_sc = tally("f_sc", F)
        f_mx = tally("f_mx", F)
        f_p = tally("f_p", F, 2)
        f_tp = tally("f_tp", F, 2)
        f_pt = tally("f_pt", F, 2)
        f_pv = tally("f_pv", F, 2)
        f_ri = tally("f_ri", TT, 2)
        f_on = tally("f_on", TT)
        f_ot = tally("f_ot", TT)
        f_oe = tally("f_oe", TT, 2)
        f_y = tally("f_y", 1)
        f_s = tally("f_s", 1, 1)
        lt_ready = tally("lt_ready", 1)
        xs_ready = tally("xs_ready", 1)
        proj_ready = tally("proj_ready", QKJOBS)
        sq_ready = tally("sq_ready", QKJOBS, 1)
        n2_ready = tally("n2_ready", QKJOBS, 1)
        n2_max = tally("n2_max", QKJOBS)
        rs_step = tally("rs_step", QKJOBS * RSQRT_STEPS)
        rot_ready = tally("rot_ready", QKJOBS, 1)
        sum_ready = tally("sum_ready", QKJOBS)
        r_ready = tally("r_ready", QKJOBS, 1)
        turn_ready = tally("turn_ready", QKJOBS, 1)
        turn_out = tally("turn_out", QKJOBS, 1)
        v_ready = tally("v_ready", NT)
        v_out = tally("v_out", NT, 1)
        sc_ready = tally("sc_ready", UNITS)
        mx_ready = tally("mx_ready", UNITS, 2)
        p_ready = tally("p_ready", UNITS, 2)
        tp_ready = tally("tp_ready", UNITS, 2)
        pt_ready = tally("pt_ready", UNITS, 2)
        pv_ready = tally("pv_ready", UNITS, 2)
        ri_ready = tally("ri_ready", 2 * NT, 2)
        on_ready = tally("on_ready", 2 * NT, 2)
        ot_ready = tally("ot_ready", 2 * NT, 2)
        ot_out = tally("ot_out", 2 * NT, 2)
        y_ready = tally("y_ready", 1, 1)
        x_attn = tally("x_attn", 1, 1)
        xm_ready = tally("xm_ready", 1)
        mean_ready = tally("mean_ready", 1, 1)
        xc_ready = tally("xc_ready", 1, 1)
        xc2_ready = tally("xc2_ready", 1)
        var_ready = tally("var_ready", 1, 1)
        rstd_ready = tally("rstd_ready", 1)
        wide_ready = tally("wide_ready", 1)
        ln_step = tally("ln_step", 1 + RSQRT_STEPS + 1)
        xn_ready = tally("xn_ready", 1, 1)
        up_ready = tally("up_ready", 6)
        gate_ready = tally("gate_ready", 3, 3)
        hid_ready = tally("hid_ready", 3, 3)
        down_ready = tally("down_ready", 1, 1)
        x_ffn = tally("x_ffn", 1, NSEQ)
        e_g, e_r, e_t, e_o = sem("e_g"), sem("e_r"), sem("e_t"), sem("e_o")

        block = ctx.enter_context(nc.Block())
        up_bank = [sc[:, 0, :], pj[:, 0, :], sc[:, 1, :], pj[:, 1, :], tp[:, 1, :], ob[:, 1, :]]
        W2_AT, VEC_AT = 2 * FF, 2 * FF + 3 * D
        NCONST = 16 * 5

        @block.sync
        def _(sp):
            sp.dma_start(xtok.rearrange("p (n c) -> p n c", c=D),
                         x_in.rearrange("(n p) c -> p n c", p=128)).then_inc(x_loaded, 16)
            for dst, src in ((ident[:, :], ident_in), (maskf[:, :, :], mask_in), (wqk1[:, :, :], wqk1_in),
                             (wvo1[:, :, :], wvo1_in), (bo[:, :], bo_in)):
                sp.dma_start(dst, src).then_inc(const_in, 16)
            sp.dma_start(table[:, :, :, :], table_in).then_inc(table_in_s, 16)
            sp.dma_start(qkscale[:, :], qkscale_in).then_inc(table_in_s, 16)
            sp.dma_start(wattn[:, :], wattn_in[0:128, :]).then_inc(wattn_in_s, 16)
            sp.dma_start(wffn[:, :], wffn_in[0:128, :]).then_inc(wffn_in_s, 16)
            with sp.Fori(1, DEPTH) as l:
                sp.wait_ge(y_ready.sem, y_ready.at(l - 1, NSEQ - 1, 0))
                sp.dma_start(wattn[:, :], wattn_in[ds(l * 128, 128), :]).then_inc(wattn_in_s, 16)
                sp.wait_ge(x_ffn.sem, x_ffn.at(l - 1, NSEQ - 1, 0))
                sp.dma_start(wffn[:, :], wffn_in[ds(l * 128, 128), :]).then_inc(wffn_in_s, 16)
            sp.wait_ge(y_ready.sem, y_ready.at(DEPTH - 1, NSEQ - 1, 0))
            sp.dma_start(xtok.rearrange("p (n c) -> p n c", c=D),
                         x_in.rearrange("(n p) c -> p n c", p=128)).then_inc(xtok_loaded, 16)
            for b in range(NSEQ):
                sp.wait_ge(e_o, b + 1)
                sp.dma_start(out.rearrange("(n p) c -> p n c", p=128)[:, TT * b:TT * (b + 1), :],
                             qT[:, b, :].rearrange("p (t c) -> p t c", t=TT)).then_inc(stored, 16)
            sp.wait_ge(stored, 16 * NSEQ)

        @block.gpsimd
        def _(pool):
            nc.gpsimd.memset(xs[:, :], 0.0).then_inc(zero_ready, 1)
            nc.gpsimd.memset(xm[:, :], 0.0).then_inc(zero_ready, 1)
            nc.gpsimd.memset(kT[:, :, 0:W], 0.0).then_inc(zero_ready, 1)
            nc.gpsimd.memset(mean_w[:, :], 1.0 / D).then_inc(zero_ready, 1)
            nc.gpsimd.memset(ones[:, :], 1.0).then_inc(zero_ready, 1)
            pool.sem_inc(r_ready.sem, 1)
            pool.wait_ge(zero_ready, 5)

            def qk_job(l, b, j):
                pool.wait_ge(rot_ready.sem, rot_ready.at(l, b, j))
                nc.gpsimd.tensor_tensor(rot[:, :], rot[:, :], rot_s[:, :], ALU.add).then_inc(sum_ready.sem, 1)
                pool.wait_ge(sum_ready.sem, sum_ready.at(l, b, j))
                pool.wait_ge(rs_step.sem, rs_step.at(l, b, (j + 1) * RSQRT_STEPS - 1))
                r3 = rot[:, :].rearrange("p (h d) -> p h d", d=DH)
                nc.gpsimd.tensor_tensor(r3, r3, rn[:, j % 2, :].unsqueeze(2).broadcast_to([128, H, DH]),
                                        ALU.mult).then_inc(r_ready.sem, 1)

            def units(l, b, own, following):
                for slot in range(UNITS):
                    for kind, j, ahead in jobs_at(slot, own, following):
                        if kind == "proj":
                            qk_job(l, b + ahead, j)

            pool.wait_ge(f_s.sem, f_s.at(0, NSEQ - 1, 0))
            with pool.Fori(0, DEPTH) as l:
                for slot in range(UNITS):
                    for kind, j, _ in jobs_at(slot, False, True):
                        if kind == "proj":
                            qk_job(l, 0, j)
                with pool.Fori(0, NSEQ - 1) as b:
                    units(l, b, True, True)
                units(l, NSEQ - 1, True, False)

        @block.scalar
        def _(act):
            act.wait_ge(const_in, NCONST)
            nc.scalar.copy(ident_b[:, :], ident[:, :]).then_inc(const_ready, 1)
            nc.scalar.copy(mask[:, :, :], maskf[:, :, :]).then_inc(const_ready, 1)
            for t in (f_pe, f_p, f_oe, f_s, sq_ready, turn_out, v_out, p_ready, ot_out, gate_ready):
                act.sem_inc(t.sem, t.head_start)

            with act.Fori(0, NSEQ) as b:
                act.wait_ge(f_xt.sem, f_xt.at(0, b, 0))
                nc.scalar.copy(x[:, ds(b * S, S)], ob[:, 0, :])
                nc.scalar.copy(xb, ob[:, 0, :]).then_inc(f_x.sem, 1)
                for n in range(9):
                    act.wait_ge(f_pj.sem, f_pj.at(0, b, n))
                    src = pj[:, n % 2, :]
                    if n < 4:
                        nc.scalar.mul(qT1[:, n, :], src, float(CH) ** -0.5).then_inc(f_pe.sem, 1)
                    elif n < 8:
                        nc.scalar.copy(kT1[:, n - 4, :], src).then_inc(f_pe.sem, 1)
                    else:
                        nc.scalar.copy(v1, src.rearrange("p (t c) -> p t c", t=TT)).then_inc(f_pe.sem, 1)

                def turned(t):
                    act.wait_ge(f_ot.sem, f_ot.at(0, b, t))
                    nc.scalar.copy(oT1[:, 128 * t:128 * t + 128], ob[:, t % 2, 128:256]).then_inc(f_oe.sem, 1)

                for u in range(F):
                    t, h = u // H, u % H
                    nk = 128 * (t + 1)
                    act.wait_ge(f_mx.sem, f_mx.at(0, b, u))
                    act.wait_ge(f_tp.sem, f_tp.at(0, b, u - 2))
                    if h == 0:
                        act.wait_ge(f_ri.sem, f_ri.at(0, b, t - 2))
                    nc.scalar.activation(p[:, u % 2, 0:nk], sc[:, u % 2, 0:nk], ACT.Exp,
                                         bias=nmax[:, u % 2, 0:1],
                                         accum_out=psums[:, t % 2, h:h + 1]).then_inc(f_p.sem, 1)
                    if h == 6 and t > 0:
                        turned(t - 1)
                turned(TT - 1)
                act.wait_ge(f_y.sem, f_y.at(0, b, 0))
                nc.scalar.activation(sa[:, ds(b * S, S)], ob[:, 0, :], ACT.Identity, bias=bo[:, 0:1]).then_inc(f_s.sem, 1)

            with act.Fori(0, DEPTH) as l:
                def job(b, kind, j):
                    if kind == "proj":
                        act.wait_ge(proj_ready.sem, proj_ready.at(l, b, j))
                        act.wait_ge(n2_ready.sem, n2_ready.at(l, b, j - 1))
                        nc.scalar.activation(sq[:, :], pj[:, :, :].rearrange("p a b -> p (a b)"),
                                             ACT.Square).then_inc(sq_ready.sem, 1)
                    elif kind == "turn":
                        act.wait_ge(turn_ready.sem, turn_ready.at(l, b, j))
                        tau = j // 2
                        dst = (kT[:, :, W + 128 * tau:W + 128 * tau + 128] if j % 2 else
                               qT[:, :, 128 * tau:128 * tau + 128])
                        nc.scalar.copy(dst, pj[:, :, :].rearrange("p a (i c) -> p (a i) c", c=128)
                                       ).then_inc(turn_out.sem, 1)
                    else:
                        act.wait_ge(v_ready.sem, v_ready.at(l, b, j))
                        nk = tile_keys(j)
                        nc.scalar.copy(v[0:nk, j, :], pj[0:nk, :, :].rearrange("p a b -> p (a b)")
                                       ).then_inc(v_out.sem, 1)

                def exps(b, n):
                    t, half, par = n // 4, n % 4 // 2, n % 2
                    mq, nk = tile_queries(t), tile_keys(t)
                    act.wait_ge(mx_ready.sem, mx_ready.at(l, b, n))
                    act.wait_ge(tp_ready.sem, tp_ready.at(l, b, n - 2))
                    if par == 0:
                        act.wait_ge(ri_ready.sem, ri_ready.at(l, b, n // 2 - 2))
                    for i in range(4):
                        last = nc.scalar.activation(p[0:mq, n % 2, i * nk:(i + 1) * nk],
                                                    sc[0:mq, n % 2, i * nk:(i + 1) * nk], ACT.Exp,
                                                    bias=nmax[0:mq, n % 2, i:i + 1],
                                                    accum_out=psums[0:mq, half, 2 * i + par:2 * i + par + 1])
                    last.then_inc(p_ready.sem, 1)

                def turned(b, m):
                    t, half = m // 2, m % 2
                    mq = tile_queries(t)
                    act.wait_ge(ot_ready.sem, ot_ready.at(l, b, m))
                    nc.scalar.copy(oT[:, 4 * half:4 * half + 4, QT * t:QT * t + mq],
                                   ob[:, half, 0:4 * mq].rearrange("p (i c) -> p i c", i=4)).then_inc(ot_out.sem, 1)

                def units(b, own, following):
                    for slot in range(UNITS + 5):
                        if slot < UNITS:
                            exps(b, slot)
                        if slot >= 5 and (slot - 5) % 2 == 0:
                            turned(b, (slot - 5) // 2)
                        for kind, j, ahead in jobs_at(slot, own, following):
                            job(b + ahead, kind, j)

                for slot in range(UNITS):
                    for kind, j, _ in jobs_at(slot, False, True):
                        job(0, kind, j)
                with act.Fori(0, NSEQ - 1) as b:
                    units(b, True, True)
                units(NSEQ - 1, True, False)

                def square(b):
                    act.wait_ge(xc_ready.sem, xc_ready.at(l, b, 0))
                    act.wait_ge(var_ready.sem, var_ready.at(l, b, -1))
                    nc.scalar.activation(xc2[:, :], xc[:, :], ACT.Square).then_inc(xc2_ready.sem, 1)

                def gelus(b):
                    for c in range(3):
                        rows = CHUNK[c]
                        act.wait_ge(up_ready.sem, up_ready.at(l, b, 2 * c))
                        act.wait_ge(hid_ready.sem, hid_ready.at(l, b, c - 3))
                        nc.scalar.activation(gate[0:rows, c, :], up_bank[2 * c][0:rows, :], ACT.Gelu,
                                             bias=wffn[0:rows, VEC_AT + 6 + c:VEC_AT + 7 + c]).then_inc(gate_ready.sem, 1)

                act.wait_ge(wffn_in_s, (l + 1) * 16)
                square(0)
                with act.Fori(0, NSEQ - 1) as b:
                    square(b + 1)
                    gelus(b)
                gelus(NSEQ - 1)

            for b in range(NSEQ):
                act.wait_ge(x_ffn.sem, x_ffn.at(DEPTH - 1, b, 0))
                nc.scalar.activation(x[:, b * S:(b + 1) * S], x[:, b * S:(b + 1) * S], ACT.Silu).then_inc(e_g, 1)

        @block.vector
        def _(dve):
            for t in (f_pt, f_ri, n2_ready, rot_ready, mx_ready, pt_ready, ri_ready, on_ready,
                      x_attn, xc_ready, xn_ready, hid_ready, x_ffn):
                dve.sem_inc(t.sem, t.head_start)

            def shifted(dst, src_at):
                nc.vector.tensor_copy(dst[0:64, 0:S], x[0:64, ds(src_at, S)])
                return nc.vector.tensor_copy(dst[64:128, 1:S], x[64:128, ds(src_at, S - 1)])

            def rsqrt(link, y, n, tmp):
                i32 = mybir.dt.int32
                link(nc.vector.tensor_scalar(tmp.bitcast(i32), n.bitcast(i32), 1, None, ALU.logical_shift_right))
                link(nc.vector.tensor_scalar(y.bitcast(i32), tmp.bitcast(i32), -1.0, MAGIC, ALU.mult, ALU.add))
                for _ in range(NEWTON):
                    link(nc.vector.scalar_tensor_tensor(out=tmp, in0=y, scalar=-0.5, in1=y, op0=ALU.mult, op1=ALU.mult))
                    link(nc.vector.tensor_tensor(tmp, tmp, n, ALU.mult))
                    link(nc.vector.scalar_tensor_tensor(out=y, in0=tmp, scalar=1.5, in1=y, op0=ALU.add, op1=ALU.mult))

            dve.wait_ge(zero_ready, 5)
            dve.wait_ge(x_loaded, 16)
            with dve.Fori(0, NSEQ) as b:
                step = 0

                def link(ins):
                    nonlocal step
                    ins.then_inc(f_ln.sem, 1)
                    dve.wait_ge(f_ln.sem, f_ln.at(0, b, step))
                    step += 1

                xt = xtok[:, ds(b * S, S)].rearrange("p (t c) -> p t c", t=TT)
                wide = lambda a: a.unsqueeze(2).broadcast_to([128, TT, D])
                link(nc.vector.reduce_sum(st[:, 0, :], xt, AX.X))
                link(nc.vector.tensor_scalar(st[:, 1, :], st[:, 0, :], 1.0 / D, None, ALU.mult))
                link(nc.vector.tensor_tensor(xtc, xt, wide(st[:, 1, :]), ALU.subtract))
                link(nc.vector.tensor_tensor(xtq, xtc, xtc, ALU.mult))
                link(nc.vector.reduce_sum(st[:, 2, :], xtq, AX.X))
                link(nc.vector.tensor_scalar(st[:, 3, :], st[:, 2, :], 1.0 / D, EPS, ALU.mult, ALU.add))
                rsqrt(link, st[:, 4, :], st[:, 3, :], st[:, 5, :])
                nc.vector.tensor_tensor(xtn, xtc, wide(st[:, 4, :]), ALU.mult).then_inc(f_xn.sem, 1)

                def top(u):
                    nk = 128 * (u // H + 1)
                    dve.wait_ge(f_sc.sem, f_sc.at(0, b, u))
                    dve.wait_ge(f_p.sem, f_p.at(0, b, u - 2))
                    nc.vector.reduce_max(nmax[:, u % 2, 0:1], sc[:, u % 2, 0:nk], AX.X, negate=True).then_inc(f_mx.sem, 1)

                def copy_pt(u):
                    nk = 128 * (u // H + 1)
                    dve.wait_ge(f_tp.sem, f_tp.at(0, b, u))
                    dve.wait_ge(f_pv.sem, f_pv.at(0, b, u - 2))
                    nc.vector.tensor_copy(pT[:, u % 2, 0:nk], tp[:, u % 2, 0:nk]).then_inc(f_pt.sem, 1)

                def normalise(t):
                    dve.wait_ge(f_p.sem, f_p.at(0, b, H * (t + 1) - 1))
                    nc.vector.reciprocal(rinv[:, t % 2, :], psums[:, t % 2, :]).then_inc(f_ri.sem, 1)
                    dve.wait_ge(f_ri.sem, f_ri.at(0, b, t))
                    dve.wait_ge(f_pv.sem, f_pv.at(0, b, H * (t + 1) - 1))
                    nc.vector.tensor_tensor(osb[:, t % 2, 0:D].rearrange("p (h c) -> p h c", h=H),
                                            ob[:, t % 2, 0:D].rearrange("p (h c) -> p h c", h=H),
                                            rinv[:, t % 2, :].unsqueeze(2).broadcast_to([128, H, CH]),
                                            ALU.mult).then_inc(f_on.sem, 1)

                for slot in range(F + 3):
                    if slot < F:
                        top(slot)
                    if 1 <= slot <= F:
                        copy_pt(slot - 1)
                    if slot >= 3 and (slot - 3) % H == H - 1:
                        normalise((slot - 3) // H)

            dve.wait_ge(f_s.sem, f_s.at(0, NSEQ - 1, 0))
            dve.wait_ge(const_in, NCONST)
            dve.wait_ge(table_in_s, 32)
            with dve.Fori(0, DEPTH) as l:
                nc.vector.tensor_tensor(ltable[:, :, :, :], table[:, :, :, :],
                                        qkscale[:, ds(l * (4 * DH), 4 * DH)].rearrange("p (k d) -> p k d", k=4)
                                        .unsqueeze(2).broadcast_to([128, 4, TT, DH]), ALU.mult).then_inc(lt_ready.sem, 1)
                dve.wait_ge(lt_ready.sem, l + 1)

                def load_xs(b, first=False):
                    dve.wait_ge(x_ffn.sem, x_ffn.at(l - 1, b, 0))
                    if not first:
                        dve.wait_ge(proj_ready.sem, proj_ready.at(l, b, -1))
                        dve.wait_ge(v_ready.sem, v_ready.at(l, b, -1))
                    shifted(xs[:, W:W + S], b * S).then_inc(xs_ready.sem, 1)

                def qk_job(b, j):
                    tau, kind = j // 2, j % 2
                    dve.wait_ge(sq_ready.sem, sq_ready.at(l, b, j))
                    dve.wait_ge(r_ready.sem, r_ready.at(l, b, j - 1))
                    dve.wait_ge(turn_ready.sem, turn_ready.at(l, b, j - 1))
                    src = pj[:, :, :].rearrange("p a (h d) -> p (a h) d", d=DH)
                    a3 = rot[:, :].rearrange("p (h d) -> p h d", d=DH)
                    b3 = rot_s[:, :].rearrange("p (h d) -> p h d", d=DH)
                    tab = lambda k, lo, hi: (ltable[:, k, tau, lo:hi].unsqueeze(1)
                                             .broadcast_to([128, H, hi - lo]))
                    nc.vector.tensor_tensor(a3, src, tab(2 * kind, 0, DH), ALU.mult)
                    hd = DH // 2
                    nc.vector.tensor_tensor(b3[:, :, 0:hd], src[:, :, hd:DH], tab(2 * kind + 1, 0, hd), ALU.mult)
                    nc.vector.tensor_tensor(b3[:, :, hd:DH], src[:, :, 0:hd], tab(2 * kind + 1, hd, DH),
                                            ALU.mult).then_inc(rot_ready.sem, 1)
                    nc.vector.reduce_sum(n2[:, :], sq[:, :].rearrange("p (h d) -> p h d", d=DH), AX.X).then_inc(n2_ready.sem, 1)
                    dve.wait_ge(n2_ready.sem, n2_ready.at(l, b, j))
                    step = j * RSQRT_STEPS

                    def link(ins):
                        nonlocal step
                        ins.then_inc(rs_step.sem, 1)
                        dve.wait_ge(rs_step.sem, rs_step.at(l, b, step))
                        step += 1

                    nc.vector.tensor_scalar(rtmp[:, 1, :], n2[:, :], 1e-24, None, ALU.max).then_inc(n2_max.sem, 1)
                    dve.wait_ge(n2_max.sem, n2_max.at(l, b, j))
                    dve.wait_ge(r_ready.sem, r_ready.at(l, b, j - 1))
                    rsqrt(link, rn[:, j % 2, :], rtmp[:, 1, :], rtmp[:, 0, :])

                def top(b, n):
                    mq, nk = tile_queries(n // 4), tile_keys(n // 4)
                    dve.wait_ge(sc_ready.sem, sc_ready.at(l, b, n))
                    dve.wait_ge(p_ready.sem, p_ready.at(l, b, n - 2))
                    nc.vector.reduce_max(nmax[0:mq, n % 2, :],
                                         sc[0:mq, n % 2, 0:4 * nk].rearrange("p (i k) -> p i k", i=4),
                                         AX.X, negate=True).then_inc(mx_ready.sem, 1)

                def copy_pt(b, n):
                    mq, nk = tile_queries(n // 4), tile_keys(n // 4)
                    dve.wait_ge(tp_ready.sem, tp_ready.at(l, b, n))
                    dve.wait_ge(pv_ready.sem, pv_ready.at(l, b, n - 2))
                    nc.vector.tensor_copy(pT[0:nk, n % 2, 0:4 * mq], tp[0:nk, n % 2, 0:4 * mq]).then_inc(pt_ready.sem, 1)

                def normalise(b, m):
                    mq = tile_queries(m // 2)
                    half = m % 2
                    dve.wait_ge(p_ready.sem, p_ready.at(l, b, 2 * m + 1))
                    nc.vector.reciprocal(rinv[0:mq, half, 0:8], psums[0:mq, half, 0:8]).then_inc(ri_ready.sem, 1)
                    dve.wait_ge(ri_ready.sem, ri_ready.at(l, b, m))
                    dve.wait_ge(pv_ready.sem, pv_ready.at(l, b, 2 * m + 1))
                    dve.wait_ge(ot_ready.sem, ot_ready.at(l, b, m - 2))
                    nc.vector.tensor_tensor(osb[0:mq, half, :].rearrange("p (h c) -> p h c", h=8),
                                            ob[0:mq, half, :].rearrange("p (h c) -> p h c", h=8),
                                            rinv[0:mq, half, 0:8].unsqueeze(2).broadcast_to([mq, 8, DH]),
                                            ALU.mult).then_inc(on_ready.sem, 1)

                def units(b, own, following):
                    for slot in range(UNITS + 3):
                        if following and slot == PROJ_SLOT[0] - 2:
                            load_xs(b + 1)
                        if slot < UNITS:
                            top(b, slot)
                        if 1 <= slot <= UNITS:
                            copy_pt(b, slot - 1)
                        if slot >= 4 and slot % 2 == 0:
                            normalise(b, (slot - 4) // 2)
                        for kind, j, ahead in jobs_at(slot, own, following):
                            if kind == "proj":
                                qk_job(b + ahead, j)
                    dve.wait_ge(y_ready.sem, y_ready.at(l, b, 0))
                    nc.vector.tensor_tensor(x[:, ds(b * S, S)], ob[:, 0, :], x[:, ds(b * S, S)],
                                            ALU.add).then_inc(x_attn.sem, 1)

                load_xs(0, first=True)
                for slot in range(UNITS):
                    for kind, j, _ in jobs_at(slot, False, True):
                        if kind == "proj":
                            qk_job(0, j)
                dve.sem_inc(waits_past, 1)
                with dve.Fori(0, NSEQ - 1) as b:
                    units(b, True, True)
                units(NSEQ - 1, True, False)

                def load_xm(b):
                    dve.wait_ge(x_attn.sem, x_attn.at(l, b, 0))
                    dve.wait_ge(mean_ready.sem, mean_ready.at(l, b, -1))
                    shifted(xm[:, :], b * S).then_inc(xm_ready.sem, 1)

                def centre(b):
                    dve.wait_ge(mean_ready.sem, mean_ready.at(l, b, 0))
                    nc.vector.tensor_tensor(xc[:, :], xm[:, :], tp[:, 0, :], ALU.subtract).then_inc(xc_ready.sem, 1)

                def norm(b):
                    step = 0

                    def link(ins):
                        nonlocal step
                        ins.then_inc(ln_step.sem, 1)
                        dve.wait_ge(ln_step.sem, ln_step.at(l, b, step))
                        step += 1

                    dve.wait_ge(var_ready.sem, var_ready.at(l, b, 0))
                    link(nc.vector.tensor_scalar(rstd[:, 0, :], tp[:, 0, 0:TT], EPS, None, ALU.add))
                    rsqrt(link, rstd[:, 1, :], rstd[:, 0, :], rstd[:, 2, :])
                    for t in range(TT):
                        last = nc.vector.tensor_scalar(diag[:, 128 * t:128 * t + 128], ident[:, :],
                                                       rstd[:, 1, t:t + 1], None, ALU.mult)
                    last.then_inc(rstd_ready.sem, 1)
                    dve.wait_ge(wide_ready.sem, wide_ready.at(l, b, 0))
                    link(nc.vector.tensor_tensor(xd[:, :], xc[:, :], tp[:, 0, :], ALU.mult))
                    nc.vector.tensor_scalar(xn[:, :], xd[:, :], wffn[:, VEC_AT:VEC_AT + 1],
                                            wffn[:, VEC_AT + 1:VEC_AT + 2], ALU.mult, ALU.add).then_inc(xn_ready.sem, 1)

                def hidden(b):
                    for c in range(3):
                        rows = CHUNK[c]
                        dve.wait_ge(up_ready.sem, up_ready.at(l, b, 2 * c + 1))
                        dve.wait_ge(gate_ready.sem, gate_ready.at(l, b, c))
                        dve.wait_ge(down_ready.sem, down_ready.at(l, b, -1))
                        nc.vector.scalar_tensor_tensor(out=hid[0:rows, c, :], in0=up_bank[2 * c + 1][0:rows, :],
                                                       scalar=wffn[0:rows, VEC_AT + 3 + c:VEC_AT + 4 + c],
                                                       in1=gate[0:rows, c, :], op0=ALU.add,
                                                       op1=ALU.mult).then_inc(hid_ready.sem, 1)

                def add_ffn(b):
                    dve.wait_ge(down_ready.sem, down_ready.at(l, b, 0))
                    nc.vector.scalar_tensor_tensor(out=x[:, ds(b * S, S)], in0=ob[:, 0, :],
                                                   scalar=wffn[:, VEC_AT + 2:VEC_AT + 3], in1=x[:, ds(b * S, S)],
                                                   op0=ALU.add, op1=ALU.add).then_inc(x_ffn.sem, 1)

                dve.wait_ge(wffn_in_s, (l + 1) * 16)
                load_xm(0)
                centre(0)
                norm(0)
                with dve.Fori(0, NSEQ - 1) as b:
                    load_xm(b + 1)
                    centre(b + 1)
                    hidden(b)
                    norm(b + 1)
                    add_ffn(b)
                hidden(NSEQ - 1)
                add_ffn(NSEQ - 1)

            dve.wait_ge(xtok_loaded, 16)
            for b in range(NSEQ + 1):
                if b < NSEQ:
                    dve.wait_ge(e_g, b + 1)
                    nc.vector.tensor_tensor(sa[:, b * S:(b + 1) * S], sa[:, b * S:(b + 1) * S],
                                            x[:, b * S:(b + 1) * S], ALU.mult).then_inc(e_r, 1)
                if b > 0:
                    dve.wait_ge(e_t, b)
                    nc.vector.tensor_tensor(qT[:, b - 1, :], tp[:, (b - 1) % 2, :],
                                            xtok[:, (b - 1) * S:b * S], ALU.add).then_inc(e_o, 1)

        @block.tensor
        def _(pe):
            pe.wait_ge(const_in, NCONST)
            pe.wait_ge(const_ready, 2)
            pe.wait_ge(zero_ready, 5)
            for t in (f_tp, f_pv, turn_ready, tp_ready, pv_ready, ot_ready, y_ready, mean_ready, var_ready, down_ready):
                pe.sem_inc(t.sem, t.head_start)
            mm, tr = nc.tensor.matmul, nc.tensor.transpose

            def short_tile(t):
                if tile_queries(t) < QT:
                    pe.sem_inc(waits_past, 1)

            with pe.Fori(0, NSEQ) as b:
                pe.wait_ge(f_xn.sem, f_xn.at(0, b, 0))
                pe.wait_ge(f_s.sem, f_s.at(0, b, -1))
                for t in range(TT):
                    last = tr(ob[:, 0, 128 * t:128 * t + 128], xtn[:, t, :], ident[:, :])
                last.then_inc(f_xt.sem, 1)
                pe.wait_ge(f_x.sem, f_x.at(0, b, 0))
                for n in range(9):
                    pe.wait_ge(f_pe.sem, f_pe.at(0, b, n - 2))
                    if n < 8:
                        last = mm(pj[:, n % 2, :], wqk1[:, n, :], xb, start=True, stop=True)
                    else:
                        for t in range(TT):
                            last = mm(pj[:, n % 2, 128 * t:128 * t + 128], xb[:, 128 * t:128 * t + 128],
                                      wvo1[:, 0, :], start=True, stop=True)
                    last.then_inc(f_pj.sem, 1)
                pe.wait_ge(f_pe.sem, f_pe.at(0, b, 8))

                def scores(u):
                    t, h = u // H, u % H
                    j, r = h % 4, 32 * (h // 4)
                    nk = 128 * (t + 1)
                    pe.wait_ge(f_p.sem, f_p.at(0, b, u - 2))
                    mm(sc[:, u % 2, 0:nk], qT1[r:r + CH, j, 128 * t:128 * t + 128], kT1[r:r + CH, j, 0:nk],
                       start=True, stop=False)
                    mm(sc[:, u % 2, nk - 128:nk], ident_b[:, :], mask[:, 2, :],
                       start=False, stop=True).then_inc(f_sc.sem, 1)

                def turn_p(u):
                    pe.wait_ge(f_p.sem, f_p.at(0, b, u))
                    pe.wait_ge(f_pt.sem, f_pt.at(0, b, u - 2))
                    for k in range(u // H + 1):
                        last = tr(tp[:, u % 2, 128 * k:128 * k + 128], p[:, u % 2, 128 * k:128 * k + 128], ident[:, :])
                    last.then_inc(f_tp.sem, 1)

                def times_v(u):
                    t, h = u // H, u % H
                    pe.wait_ge(f_pt.sem, f_pt.at(0, b, u))
                    if h == 0:
                        pe.wait_ge(f_oe.sem, f_oe.at(0, b, t - 2))
                    for k in range(t + 1):
                        last = mm(ob[:, t % 2, CH * h:CH * h + CH], pT[:, u % 2, 128 * k:128 * k + 128],
                                  v1[:, k, CH * h:CH * h + CH], start=(k == 0), stop=(k == t))
                    last.then_inc(f_pv.sem, 1)

                def turn_o(t):
                    pe.wait_ge(f_on.sem, f_on.at(0, b, t))
                    tr(ob[:, t % 2, 128:256], osb[:, t % 2, 0:D], ident[:, :]).then_inc(f_ot.sem, 1)

                for slot in range(F + 2):
                    if slot < F:
                        scores(slot)
                    if 1 <= slot <= F:
                        turn_p(slot - 1)
                    if slot >= 2:
                        times_v(slot - 2)
                    if slot >= 5 and (slot - 5) % H == H - 1:
                        turn_o((slot - 5) // H)
                turn_o(TT - 1)
                pe.wait_ge(f_oe.sem, f_oe.at(0, b, TT - 1))
                mm(ob[:, 0, :], wvo1[:, 1, :], oT1, start=True, stop=True).then_inc(f_y.sem, 1)
            pe.wait_ge(f_s.sem, f_s.at(0, NSEQ - 1, 0))

            with pe.Fori(0, DEPTH) as l:
                pe.wait_ge(x_ffn.sem, x_ffn.at(l, 0, -1))
                pe.wait_ge(wattn_in_s, (l + 1) * 16)

                def banks_free(b, kind, j):
                    k, n, back = before(kind, j)
                    if k == "proj":
                        pe.wait_ge(sq_ready.sem, sq_ready.at(l, b - back, n))
                        pe.wait_ge(rot_ready.sem, rot_ready.at(l, b - back, n))
                    elif k == "turn":
                        pe.wait_ge(turn_out.sem, turn_out.at(l, b - back, n))
                    else:
                        pe.wait_ge(v_out.sem, v_out.at(l, b - back, n))

                def job(b, kind, j, first=False):
                    if not (first and (kind, j) == ("proj", 0)):
                        banks_free(b, kind, j)
                    if kind == "proj":
                        if j == 0:
                            pe.wait_ge(xs_ready.sem, xs_ready.at(l, b, 0))
                        tau, base = j // 2, INNER * (j % 2)
                        for a in range(2):
                            last = mm(pj[:, a, :], xs[:, W + 128 * tau:W + 128 * tau + 128],
                                      wattn[:, base + 512 * a:base + 512 * a + 512], start=True, stop=True)
                        last.then_inc(proj_ready.sem, 1)
                    elif kind == "turn":
                        pe.wait_ge(r_ready.sem, r_ready.at(l, b, j))
                        for i in range(PAIRS):
                            last = tr(pj[:, i // 4, 128 * (i % 4):128 * (i % 4) + 128],
                                      rot[:, 128 * i:128 * i + 128], ident[:, :])
                        last.then_inc(turn_ready.sem, 1)
                    else:
                        nk = tile_keys(j)
                        for a in range(2):
                            last = mm(pj[0:nk, a, :], xs[:, QT * j:QT * j + nk],
                                      wattn[:, 2 * INNER + 512 * a:2 * INNER + 512 * a + 512], start=True, stop=True)
                        last.then_inc(v_ready.sem, 1)

                def scores(b, n):
                    t, half, par = n // 4, n % 4 // 2, n % 2
                    mq, nk, r = tile_queries(t), tile_keys(t), 64 * par
                    pe.wait_ge(p_ready.sem, p_ready.at(l, b, n - 2))
                    if n % 4 == 0:
                        pe.wait_ge(turn_out.sem, turn_out.at(l, b, 2 * ((QT * t + mq - 1) // 128) + 1))
                    short_tile(t)
                    for i in range(4):
                        mm(sc[0:mq, n % 2, i * nk:(i + 1) * nk], qT[r:r + DH, 4 * half + i, QT * t:QT * t + mq],
                           kT[r:r + DH, 4 * half + i, QT * t:QT * t + nk], start=(i == 0), stop=False)
                    mm(sc[0:mq, n % 2, 0:4 * nk], ident_b[0:mq, 0:mq],
                       mask[0:mq, 0 if t else 1, 0:nk].unsqueeze(1).broadcast_to([mq, 4, nk]),
                       start=False, stop=True).then_inc(sc_ready.sem, 1)

                def turn_p(b, n):
                    mq, nk = tile_queries(n // 4), tile_keys(n // 4)
                    pe.wait_ge(p_ready.sem, p_ready.at(l, b, n))
                    pe.wait_ge(pt_ready.sem, pt_ready.at(l, b, n - 2))
                    short_tile(n // 4)
                    for i in range(4):
                        last = tr(tp[0:nk, n % 2, i * mq:(i + 1) * mq], p[0:mq, n % 2, i * nk:(i + 1) * nk],
                                  ident[0:mq, 0:mq])
                    last.then_inc(tp_ready.sem, 1)

                def times_v(b, n):
                    t, half, par = n // 4, n % 4 // 2, n % 2
                    mq, nk = tile_queries(t), tile_keys(t)
                    pe.wait_ge(pt_ready.sem, pt_ready.at(l, b, n))
                    if par == 0:
                        pe.wait_ge(ot_out.sem, ot_out.at(l, b, n // 2 - 2))
                    if n == 0:
                        pe.wait_ge(x_attn.sem, x_attn.at(l, b, -1))
                    if n % 4 == 0:
                        pe.wait_ge(v_out.sem, v_out.at(l, b, t))
                    short_tile(t)
                    for i in range(4):
                        h = 8 * half + 2 * i + par
                        last = mm(ob[0:mq, half, (2 * i + par) * DH:(2 * i + par + 1) * DH],
                                  pT[0:nk, n % 2, i * mq:(i + 1) * mq], v[0:nk, t, h * DH:(h + 1) * DH],
                                  start=True, stop=True)
                    last.then_inc(pv_ready.sem, 1)

                def turn_o(b, m):
                    mq, half = tile_queries(m // 2), m % 2
                    pe.wait_ge(on_ready.sem, on_ready.at(l, b, m))
                    short_tile(m // 2)
                    for i in range(4):
                        last = tr(ob[:, half, i * mq:(i + 1) * mq], osb[0:mq, half, 128 * i:128 * i + 128],
                                  ident[0:mq, 0:mq])
                    last.then_inc(ot_ready.sem, 1)

                def units(b, own, following):
                    for slot in range(UNITS + 2):
                        if slot < UNITS:
                            scores(b, slot)
                        if 1 <= slot <= UNITS:
                            turn_p(b, slot - 1)
                        if slot >= 2:
                            times_v(b, slot - 2)
                        if slot >= 5 and (slot - 5) % 2 == 0:
                            turn_o(b, (slot - 5) // 2)
                        for kind, j, ahead in jobs_at(slot, own, following):
                            job(b + ahead, kind, j)
                    turn_o(b, 2 * NT - 1)
                    pe.wait_ge(ot_out.sem, ot_out.at(l, b, 2 * NT - 1))
                    for i in range(PAIRS):
                        last = mm(ob[:, 0, :], wattn[:, 3 * INNER + D * i:3 * INNER + D * (i + 1)], oT[:, i, :],
                                  start=(i == 0), stop=(i == PAIRS - 1))
                    last.then_inc(y_ready.sem, 1)

                for slot in range(UNITS):
                    for kind, j, _ in jobs_at(slot, False, True):
                        job(0, kind, j, first=True)
                with pe.Fori(0, NSEQ - 1) as b:
                    units(b, True, True)
                units(NSEQ - 1, True, False)

                def mean(b):
                    pe.wait_ge(xm_ready.sem, xm_ready.at(l, b, 0))
                    pe.wait_ge(xn_ready.sem, xn_ready.at(l, b, -1))
                    mm(tp[:, 0, :], mean_w[:, :], xm[:, :], start=True, stop=True).then_inc(mean_ready.sem, 1)

                def variance(b):
                    pe.wait_ge(xc2_ready.sem, xc2_ready.at(l, b, 0))
                    for t in range(TT):
                        last = mm(tp[:, 0, t:t + 1], xc2[:, 128 * t:128 * t + 128], mean_w[:, 0:1], start=True, stop=True)
                    last.then_inc(var_ready.sem, 1)

                def widen(b):
                    pe.wait_ge(rstd_ready.sem, rstd_ready.at(l, b, 0))
                    mm(tp[:, 0, :], ones[:, :], diag[:, :], start=True, stop=True).then_inc(wide_ready.sem, 1)

                def up(b):
                    pe.wait_ge(xn_ready.sem, xn_ready.at(l, b, 0))
                    for c in range(3):
                        rows = CHUNK[c]
                        for side, done in ((0, gate_ready), (1, hid_ready)):
                            pe.wait_ge(done.sem, done.at(l, b, c - 3))
                            at = FC * c + (FF if side == 0 else 0)
                            mm(up_bank[2 * c + side][0:rows, :], wffn[:, at:at + rows], xn[:, :],
                               start=True, stop=True).then_inc(up_ready.sem, 1)

                def down(b):
                    pe.wait_ge(x_ffn.sem, x_ffn.at(l, b, -1))
                    for c in range(3):
                        rows = CHUNK[c]
                        pe.wait_ge(hid_ready.sem, hid_ready.at(l, b, c))
                        last = mm(ob[:, 0, :], wffn[0:rows, W2_AT + D * c:W2_AT + D * (c + 1)], hid[0:rows, c, :],
                                  start=(c == 0), stop=(c == 2))
                    last.then_inc(down_ready.sem, 1)

                pe.wait_ge(x_attn.sem, x_attn.at(l, NSEQ - 1, 0))
                pe.wait_ge(wffn_in_s, (l + 1) * 16)
                mean(0)
                variance(0)
                widen(0)
                with pe.Fori(0, NSEQ - 1) as b:
                    mean(b + 1)
                    up(b)
                    variance(b + 1)
                    down(b)
                    widen(b + 1)
                up(NSEQ - 1)
                down(NSEQ - 1)

            for b in range(NSEQ):
                pe.wait_ge(e_r, b + 1)
                if b >= 2:
                    pe.wait_ge(e_o, b - 1)
                for t in range(TT):
                    last = tr(tp[:, b % 2, 128 * t:128 * t + 128],
                              sa[:, b * S + 128 * t:b * S + 128 * t + 128], ident[:, :])
                last.then_inc(e_t, 1)


def rotary_constants():
    half = np.arange(0, DH, 2, dtype=np.float32)
    inv_freq = (np.float32(1.0) / np.power(np.float32(10000.0), half / np.float32(DH))).astype(np.float32)
    t = np.arange(S, dtype=np.float32)
    freqs = (t[:, None] * inv_freq[None, :]).astype(np.float32)
    base = ((half + np.float32(0.4 * DH)) / np.float32(1.4 * DH)).astype(np.float32)
    power = ((t - S // 2) / np.float32(W // 2)).astype(np.float32)
    scale = base.astype(np.float64)[None, :] ** power.astype(np.float64)[:, None]
    cos, sin = np.cos(freqs.astype(np.float64)), np.sin(freqs.astype(np.float64))
    both = lambda a, b: np.concatenate([a, b], -1)
    kinds = [both(cos * scale, cos * scale) * 8.0, both(-sin * scale, sin * scale) * 8.0,
             both(cos / scale, cos / scale), both(-sin / scale, sin / scale)]
    return np.ascontiguousarray(np.stack(kinds).reshape(4, TT, 128, DH).transpose(2, 0, 1, 3)).astype(np.float32)


def mask_constants():
    r, c = np.arange(128)[:, None], np.arange(128)[None, :]
    local = np.where((c >= r) & (c <= r + W), 0.0, NEG)
    start = np.where((c >= r) & (c <= r + W) & (c >= W), 0.0, NEG)
    causal = np.where(c <= r, 0.0, NEG)
    return np.ascontiguousarray(np.stack([local, start, causal], 1)).astype(np.float32)


def kernel(**inputs):
    import concourse.bacc as bacc
    from concourse.bass_utils import run_bass_kernel_spmd

    a = {k.replace("L0_", ""): np.asarray(v) for k, v in inputs.items()}
    f32 = np.float32
    wqk1 = np.zeros((128, 2, 4, 4, 32), f32)
    for n, name in enumerate(("attn_Wq", "attn_Wk")):
        wqk1[:, n, :, :, 0:CH] = a[name].reshape(D, 4, 4, CH).transpose(0, 2, 1, 3)
    qs, ks = a["ffn_q_scale"], a["ffn_k_scale"]
    swap = lambda s: np.concatenate([s[:, DH // 2:], s[:, :DH // 2]], -1)
    scales = np.stack([qs, swap(qs), ks, swap(ks)], 1).reshape(1, DEPTH * 4 * DH)
    wattn = np.concatenate([a["ffn_Wqkv"], a["ffn_Wo"].reshape(DEPTH, PAIRS, 128, D).transpose(0, 2, 1, 3)
                            .reshape(DEPTH, 128, PAIRS * D)], -1)
    w2 = np.zeros((DEPTH, 128, 3, D), f32)
    b1 = np.zeros((DEPTH, 128, 2, 3), f32)
    for c in range(3):
        at, rows = FC * c, CHUNK[c]
        w2[:, 0:rows, c, :] = a["ffn_W2"][:, at:at + rows, :]
        b1[:, 0:rows, 0, c] = a["ffn_b1"][:, at:at + rows]
        b1[:, 0:rows, 1, c] = a["ffn_b1"][:, FF + at:FF + at + rows]
    wffn = np.concatenate([a["ffn_W1"], w2.reshape(DEPTH, 128, 3 * D), a["ffn_ln_g"][:, :, None],
                           a["ffn_ln_b"][:, :, None], a["ffn_b2"][:, :, None], b1.reshape(DEPTH, 128, 6)], -1)
    arrays = {
        "in_x": a["attn_x"].reshape(NSEQ * S, D),
        "in_table": rotary_constants(),
        "in_qkscale": np.broadcast_to(scales, (128, scales.shape[1])),
        "in_ident": np.eye(128, dtype=f32),
        "in_mask": mask_constants(),
        "in_wqk1": wqk1.reshape(128, 8, 128),
        "in_wvo1": np.stack([a["attn_Wv"], a["attn_Wo"]], 1),
        "in_bo": a["attn_bo"].reshape(D, 1),
        "in_wattn": wattn.reshape(DEPTH * 128, WCOLS),
        "in_wffn": wffn.reshape(DEPTH * 128, FCOLS),
    }
    arrays = {k: np.ascontiguousarray(v) for k, v in arrays.items()}
    nc = bacc.Bacc("TRN2", target_bir_lowering=False, num_devices=1)
    args = [nc.dram_tensor(k, v.shape, mybir.dt.float32, kind="ExternalInput").ap() for k, v in arrays.items()]
    args.append(nc.dram_tensor("out", (NSEQ * S, D), mybir.dt.float32, kind="ExternalOutput").ap())
    build(nc, *args)
    r = run_bass_kernel_spmd(nc, [arrays], core_ids=[0])
    return r.results[0]["out"].reshape(NSEQ, S, D)
```

```python
import numpy as np
import concourse.bass as bass
from concourse import mybir
from contextlib import ExitStack

NSEQ, S, D = 8, 512, 128
TT = S // 128
DEPTH = 6
H = 16
CH = D // H
DH, INNER = 64, 16 * 64
PAIRS = H // 2
W = 32
QT = 96
NT = -(-S // QT)
FF = int(D * 4 * 2 / 3)
FC = -(-FF // 3)
CHUNK = [min(FC, FF - FC * j) for j in range(3)]
EPS = 1e-5
NEG = -1.0e30
WCOLS = 3 * INNER + PAIRS * D + 4 * DH
FCOLS = 2 * FF + 3 * D + 3 + 6

UNITS = NT * 4
TURN_LAG, COPY_LAG, PV_LAG = 3, 3, 4
HALF_LAG = 6
RING = 4
TAIL = 8
QKJOBS = 2 * TT
PROJ_SLOT = [11 + 3 * j for j in range(QKJOBS)]
TURN_SLOT = [17 + 3 * j - (j % 2) for j in range(QKJOBS)]
V_SLOT = [12 + 3 * v for v in range(NT)]
OUT_SLOT = 2 * UNITS + 6
ORDER = ["turn", "proj", "norm", "late", "v", "out"]
BANKED = ("turn", "proj", "v", "out")
JOBS = sorted([(s, ORDER.index("proj"), j) for j, s in enumerate(PROJ_SLOT)]
              + [(s + 1, ORDER.index("norm"), j) for j, s in enumerate(PROJ_SLOT)]
              + [(s + 2, ORDER.index("late"), j) for j, s in enumerate(PROJ_SLOT) if j % 2]
              + [(s, ORDER.index("turn"), j) for j, s in enumerate(TURN_SLOT)]
              + [(s, ORDER.index("v"), v) for v, s in enumerate(V_SLOT)]
              + [(OUT_SLOT, ORDER.index("out"), 0)])


def tile_queries(t):
    return min(QT, S - QT * t)


def tile_keys(t):
    return min(128, S - QT * t + W)


MODES = ("prologue", "first", "mid", "last")


def slots(mode):
    return range(UNITS + (TAIL if mode == "last" else 0))


def alive(n, mode):
    return mode != "prologue" and n < UNITS and (n >= 0 or mode != "first")


def planned(mode):
    out = []
    for s, k, j in sorted(JOBS, key=lambda job: (job[0] % UNITS, job[1])):
        ahead = 1 - s // UNITS
        if mode == "mid" or (mode == "prologue" and ahead == 1) or (mode == "first" and ahead >= 0) \
                or (mode == "last" and ahead <= 0):
            out.append((s % UNITS, ORDER[k], j, ahead))
    if mode == "last":
        out.append((OUT_SLOT - UNITS, "out", 0, 0))
    return out


def jobs_at(slot, mode):
    jobs = planned(mode)
    uses = [job for job in jobs if job[1] in BANKED]
    out = []
    for job in jobs:
        if job[0] != slot:
            continue
        prev = None
        if job in uses:
            at = uses.index(job)
            if at > 0:
                _, k, n, ahead = uses[at - 1]
                prev = (k, n, job[3] - ahead)
            elif mode != "prologue":
                _, k, n, ahead = [u for u in planned("mid") if u[1] in BANKED][-1]
                prev = (k, n, job[3] - (ahead - 1))
        out.append((*job[1:], prev))
    return out


NEWTON = 3
RSQRT_STEPS = 2 + 3 * NEWTON
MAGIC = float(0x5f3759df)


class Tally:

    def __init__(self, sem, per_seq, head_start=0):
        self.sem, self.per_seq, self.head_start = sem, per_seq, head_start

    def at(self, layer, seq, n):
        return layer * (NSEQ * self.per_seq) + seq * self.per_seq + (n + 1 + self.head_start)


def build(nc, x_in, table_in, ident_in, mask_in, wqk1_in, wvo1_in, bo_in, wattn_in, wffn_in, out):
    fp32, bf16 = mybir.dt.float32, mybir.dt.bfloat16
    ALU, ACT, AX = mybir.AluOpType, mybir.ActivationFunctionType, mybir.AxisListType
    ds = bass.ds

    with ExitStack() as ctx:
        def sb(name, shape, dt=fp32):
            return ctx.enter_context(nc.sbuf_tensor(name, shape, dt))

        def sem(name):
            return ctx.enter_context(nc.semaphore(name))

        def tally(name, per_seq, head_start=0):
            return Tally(sem(name), per_seq, head_start)

        x = sb("x", [128, NSEQ * S])
        sa = sb("sa", [128, NSEQ * S])
        wattn = sb("wattn", [128, WCOLS])
        wffn = sb("wffn", [128, FCOLS])
        bo = sb("bo", [128, 1])
        ident = sb("ident", [128, 128])
        ident_b = sb("ident_b", [128, 128], bf16)
        mask = sb("mask", [128, 3, 128], bf16)
        table = sb("table", [128, 4, TT, DH])
        ltable = sb("ltable", [128, 4, TT, DH])
        mean_w = sb("mean_w", [128, 128])
        xs = sb("xs", [128, W + S])
        qT = sb("qT", [128, PAIRS, S])
        kT = sb("kT", [128, PAIRS, 2, W + S])
        v = sb("v", [128, NT, INNER])
        oT = sb("oT", [128, PAIRS, S])
        sq = sb("sq", [128, H * DH])
        maskf = sq[:, 0:384].rearrange("p (k c) -> p k c", c=128)
        rot = sb("rot", [128, 2, H * DH])
        rot_s = sb("rot_s", [128, H * DH])
        n2 = sb("n2", [128, 2, H])
        rn = sb("rn", [128, 2, H])
        rtmp = sb("rtmp", [128, 2, H])
        p = sb("p", [128, RING, 512])
        pT = sb("pT", [128, 2, 4 * QT])
        nmax = sb("nmax", [128, RING, 4])
        psums = sb("psums", [128, RING, 4])
        rinv = sb("rinv", [128, RING, 4])
        xm = sb("xm", [128, S])
        xc = sb("xc", [128, S])
        xc2 = sb("xc2", [128, S])
        rstd = sb("rstd", [128, 3, TT])
        diag = sb("diag", [128, S])
        ones = sb("ones", [128, 128])
        xn = sb("xn", [128, S])
        gate = sb("gate", [128, 3, S])
        hid = sb("hid", [128, 3, S])
        st = sb("st", [128, 6, TT])

        xtok = v[:, 0:4, :].rearrange("p a b -> p (a b)")
        oT1 = v[:, 4:6, :].rearrange("p a (b s) -> p (a b) s", s=S)
        qT1 = qT[:, 0:4, :]
        v1 = qT[:, 4:8, :]
        k1 = kT[:, :, :, :].rearrange("p a b c -> p (a b c)")[:, 0:H * S].rearrange("p (h s) -> p h s", s=S)
        pT1 = oT
        xb = xn
        wqk1 = gate[:, :, :].rearrange("p a b -> p (a b)")[:, 0:8 * 128].rearrange("p (a b) -> p a b", b=128)
        wvo1 = hid[:, 0:2, :]
        xtn = xc[:, :].rearrange("p (t c) -> p t c", t=TT)
        xtc = xc2[:, :].rearrange("p (t c) -> p t c", t=TT)
        xtq = diag[:, :].rearrange("p (t c) -> p t c", t=TT)

        pj = ctx.enter_context(nc.psum_tensor("pj", [128, 2, 512], fp32))
        sc = ctx.enter_context(nc.psum_tensor("sc", [128, 2, 512], fp32))
        tp = ctx.enter_context(nc.psum_tensor("tp", [128, 2, 512], fp32))
        ob = ctx.enter_context(nc.psum_tensor("ob", [128, 2, 512], fp32))

        const_in, table_in_s, x_loaded, xtok_loaded, stored = sem("const_in"), sem("table_loaded"), sem("x_loaded"), sem("xtok_loaded"), sem("stored")
        wattn_in_s, wffn_in_s = sem("wattn_loaded"), sem("wffn_loaded")
        waits_past = sem("waits_past")
        const_ready, zero_ready, layers_zero = sem("const_ready"), sem("zero_ready"), sem("layers_zero")
        F, G = TT * H, TT * 4
        f_ln = tally("f_ln", 6 + RSQRT_STEPS)
        f_xn = tally("f_xn", 1)
        f_xt = tally("f_xt", 1, 1)
        f_x = tally("f_x", 1)
        f_pj = tally("f_pj", 12)
        f_pe = tally("f_pe", 12, 2)
        f_pk = tally("f_pk", 4, 0)
        f_sc = tally("f_sc", F)
        f_mx = tally("f_mx", F)
        f_p = tally("f_p", F, RING)
        f_ri = tally("f_ri", F, RING)
        f_pn = tally("f_pn", F)
        f_tp = tally("f_tp", F, RING)
        f_pt = tally("f_pt", F, 2)
        f_pv = tally("f_pv", G, 2)
        f_oe = tally("f_oe", G, 2)
        f_y = tally("f_y", 1, 1)
        f_s = tally("f_s", 1, 1)
        lt_ready = tally("lt_ready", 1)
        xs_ready = tally("xs_ready", 1)
        proj_ready = tally("proj_ready", QKJOBS)
        sq_ready = tally("sq_ready", QKJOBS, 1)
        n2_ready = tally("n2_ready", QKJOBS, 1)
        n2_max = tally("n2_max", TT)
        rs_step = tally("rs_step", TT * RSQRT_STEPS, 1)
        rot_ready = tally("rot_ready", QKJOBS, 1)
        sum_ready = tally("sum_ready", QKJOBS, 1)
        r_ready = tally("r_ready", QKJOBS, 2)
        turn_ready = tally("turn_ready", QKJOBS, 2)
        turn_out = tally("turn_out", QKJOBS, 1)
        v_ready = tally("v_ready", NT)
        v_out = tally("v_out", NT, 1)
        sc_ready = tally("sc_ready", UNITS)
        mx_ready = tally("mx_ready", UNITS)
        p_ready = tally("p_ready", UNITS, RING)
        ri_ready = tally("ri_ready", UNITS, RING)
        pn_ready = tally("pn_ready", UNITS)
        tp_ready = tally("tp_ready", UNITS, RING)
        pt_ready = tally("pt_ready", UNITS, 2)
        pv_ready = tally("pv_ready", UNITS, 2)
        ot_out = tally("ot_out", 2 * NT, 2)
        y_ready = tally("y_ready", 1, 1)
        x_attn = tally("x_attn", 1, 1)
        xm_ready = tally("xm_ready", 1)
        mean_ready = tally("mean_ready", 1, 1)
        xc_ready = tally("xc_ready", 1, 1)
        xc2_ready = tally("xc2_ready", 1)
        var_ready = tally("var_ready", 1, 1)
        rstd_ready = tally("rstd_ready", 1)
        wide_ready = tally("wide_ready", 1)
        ln_step = tally("ln_step", 1 + RSQRT_STEPS + 1)
        xn_ready = tally("xn_ready", 1, 1)
        up_ready = tally("up_ready", 6)
        gate_ready = tally("gate_ready", 3, 3)
        hid_ready = tally("hid_ready", 3, 3)
        down_ready = tally("down_ready", 1, 1)
        x_ffn = tally("x_ffn", 1, NSEQ)
        e_g, e_r, e_t, e_o = sem("e_g"), sem("e_r"), sem("e_t"), sem("e_o")

        block = ctx.enter_context(nc.Block())
        up_bank = [sc[:, 0, :], pj[:, 0, :], sc[:, 1, :], pj[:, 1, :], tp[:, 1, :], ob[:, 1, :]]
        W2_AT, VEC_AT, SCALE_AT = 2 * FF, 2 * FF + 3 * D, 3 * INNER + PAIRS * D
        NZERO = 7
        XT_SLOT, NORM_SLOTS = 44, (8, 16, 24, 32)
        NCONST = 16 * 5

        @block.sync
        def _(sp):
            sp.dma_start(xtok.rearrange("p (n c) -> p n c", c=D),
                         x_in.rearrange("(n p) c -> p n c", p=128)).then_inc(x_loaded, 16)
            for dst, src in ((ident[:, :], ident_in), (maskf[:, :, :], mask_in), (wqk1, wqk1_in),
                             (wvo1, wvo1_in), (bo[:, :], bo_in)):
                sp.dma_start(dst, src).then_inc(const_in, 16)
            sp.dma_start(table[:, :, :, :], table_in).then_inc(table_in_s, 16)
            sp.dma_start(wattn[:, :], wattn_in[0:128, :]).then_inc(wattn_in_s, 16)
            sp.dma_start(wffn[:, :], wffn_in[0:128, :]).then_inc(wffn_in_s, 16)
            with sp.Fori(1, DEPTH) as l:
                sp.wait_ge(y_ready.sem, y_ready.at(l - 1, NSEQ - 1, 0))
                sp.dma_start(wattn[:, :], wattn_in[ds(l * 128, 128), :]).then_inc(wattn_in_s, 16)
                sp.wait_ge(x_ffn.sem, x_ffn.at(l - 1, NSEQ - 1, 0))
                sp.dma_start(wffn[:, :], wffn_in[ds(l * 128, 128), :]).then_inc(wffn_in_s, 16)
            sp.wait_ge(y_ready.sem, y_ready.at(DEPTH - 1, NSEQ - 1, 0))
            sp.dma_start(xtok.rearrange("p (n c) -> p n c", c=D),
                         x_in.rearrange("(n p) c -> p n c", p=128)).then_inc(xtok_loaded, 16)
            for b in range(NSEQ):
                sp.wait_ge(e_o, b + 1)
                sp.dma_start(out.rearrange("(n p) c -> p n c", p=128)[:, TT * b:TT * (b + 1), :],
                             qT[:, b, :].rearrange("p (t c) -> p t c", t=TT)).then_inc(stored, 16)
            sp.wait_ge(stored, 16 * NSEQ)

        @block.gpsimd
        def _(pool):
            nc.gpsimd.memset(xs[:, :], 0.0).then_inc(zero_ready, 1)
            nc.gpsimd.memset(xm[:, :], 0.0).then_inc(zero_ready, 1)
            nc.gpsimd.memset(p[:, :, :], 0.0).then_inc(zero_ready, 1)
            nc.gpsimd.memset(rinv[:, :, :], 1.0).then_inc(zero_ready, 1)
            nc.gpsimd.memset(mean_w[:, :], 1.0 / D).then_inc(zero_ready, 1)
            nc.gpsimd.memset(ones[:, :], 1.0).then_inc(zero_ready, 1)
            nc.gpsimd.memset(kT[:, :, :, :], 0.0).then_inc(zero_ready, 1)
            for t in (r_ready, sum_ready):
                pool.sem_inc(t.sem, t.head_start)
            pool.wait_ge(zero_ready, NZERO)

            with pool.Fori(0, NSEQ) as b:
                for u in range(F):
                    nk = 128 * (u // H + 1)
                    pool.wait_ge(f_ri.sem, f_ri.at(0, b, u))
                    nc.gpsimd.tensor_tensor(p[:, u % RING, 0:nk], p[:, u % RING, 0:nk],
                                            rinv[:, u % RING, 0:1].broadcast_to([128, nk]), ALU.mult).then_inc(f_pn.sem, 1)

            pool.wait_ge(f_s.sem, f_s.at(0, NSEQ - 1, 0))
            nc.gpsimd.memset(kT[:, :, :, :], 0.0).then_inc(layers_zero, 1)

            with pool.Fori(0, DEPTH) as l:
                def probabilities(b, n):
                    pool.wait_ge(ri_ready.sem, ri_ready.at(l, b, n))
                    nk = tile_keys(n % UNITS // 4)
                    p3 = p[:, n % RING, 0:4 * nk].rearrange("p (i k) -> p i k", i=4)
                    nc.gpsimd.tensor_tensor(p3, p3, rinv[:, n % RING, :].unsqueeze(2).broadcast_to([128, 4, nk]),
                                            ALU.mult).then_inc(pn_ready.sem, 1)

                def unit_norm(b, j):
                    pool.wait_ge(sum_ready.sem, sum_ready.at(l, b, j))
                    pool.wait_ge(rs_step.sem, rs_step.at(l, b, (j // 2 + 1) * RSQRT_STEPS - 1))
                    r3 = rot[:, j % 2, :].rearrange("p (h d) -> p h d", d=DH)
                    nc.gpsimd.tensor_tensor(r3, r3, rn[:, j % 2, :].unsqueeze(2).broadcast_to([128, H, DH]),
                                            ALU.mult).then_inc(r_ready.sem, 1)

                def job(b, kind, j):
                    if kind == "proj":
                        pool.wait_ge(rot_ready.sem, rot_ready.at(l, b, j))
                        nc.gpsimd.tensor_tensor(rot[:, j % 2, :], rot[:, j % 2, :], rot_s[:, :],
                                                ALU.add).then_inc(sum_ready.sem, 1)
                    elif kind == "norm" and j % 2:
                        unit_norm(b, j - 1)
                    elif kind == "late":
                        unit_norm(b, j)

                def body(b, mode):
                    for slot in slots(mode):
                        n = slot - 1
                        if alive(n, mode):
                            probabilities(b, n)
                        for kind, j, ahead, _ in jobs_at(slot, mode):
                            job(b + ahead, kind, j)

                body(-1, "prologue")
                body(0, "first")
                with pool.Fori(1, NSEQ - 1) as b:
                    body(b, "mid")
                body(NSEQ - 1, "last")

                def square(b):
                    pool.wait_ge(xc_ready.sem, xc_ready.at(l, b, 0))
                    pool.wait_ge(var_ready.sem, var_ready.at(l, b, -1))
                    nc.gpsimd.tensor_tensor(xc2[:, :], xc[:, :], xc[:, :], ALU.mult).then_inc(xc2_ready.sem, 1)

                square(0)
                with pool.Fori(0, NSEQ - 1) as b:
                    square(b + 1)

        @block.scalar
        def _(act):
            act.wait_ge(const_in, NCONST)
            nc.scalar.copy(ident_b[:, :], ident[:, :]).then_inc(const_ready, 1)
            nc.scalar.copy(mask[:, :, :], maskf[:, :, :]).then_inc(const_ready, 1)
            for t in (f_pe, f_p, f_oe, f_s, sq_ready, turn_out, v_out, p_ready, ot_out, gate_ready):
                act.sem_inc(t.sem, t.head_start)
            act.wait_ge(zero_ready, NZERO)

            def to_x(b):
                act.wait_ge(f_xt.sem, f_xt.at(0, b, 0))
                nc.scalar.copy(x[:, ds(b * S, S)], pj[:, 0, :])
                nc.scalar.copy(xb[:, :], pj[:, 0, :]).then_inc(f_x.sem, 1)

            def f_body(b, last):
                for n in range(12):
                    act.wait_ge(f_pj.sem, f_pj.at(0, b, n))
                    src = pj[:, n % 2, :]
                    if n < 4:
                        nc.scalar.mul(qT1[:, n, :], src, float(CH) ** -0.5).then_inc(f_pe.sem, 1)
                    elif n < 8:
                        for r in range(2):
                            done = nc.scalar.copy(k1[32 * r:32 * r + 32, 4 * (n - 4) + r, :], src[32 * r:32 * r + 32, :])
                        done.then_inc(f_pe.sem, 1)
                    else:
                        nc.scalar.copy(v1[:, n - 8, :], src).then_inc(f_pe.sem, 1)

                def group_out(g):
                    act.wait_ge(f_pv.sem, f_pv.at(0, b, g))
                    if g == 0:
                        act.wait_ge(f_y.sem, f_y.at(0, b, -1))
                    t, jj = g // 4, g % 4
                    nc.scalar.copy(oT1[:, jj, 128 * t:128 * t + 128], ob[:, g % 2, 0:128]).then_inc(f_oe.sem, 1)

                for slot in range(F + 5):
                    if slot < F:
                        u = slot
                        nk = 128 * (u // H + 1)
                        act.wait_ge(f_mx.sem, f_mx.at(0, b, u))
                        act.wait_ge(f_tp.sem, f_tp.at(0, b, u - RING))
                        nc.scalar.activation(p[:, u % RING, 0:nk], sc[:, u % 2, 0:nk], ACT.Exp,
                                             bias=nmax[:, u % RING, 0:1],
                                             accum_out=psums[:, u % RING, 0:1]).then_inc(f_p.sem, 1)
                    if slot >= 8 and slot % 4 == 0:
                        group_out((slot - 8) // 4)
                    if slot == XT_SLOT + 1 and not last:
                        to_x(b + 1)
                act.wait_ge(f_y.sem, f_y.at(0, b, 0))
                nc.scalar.activation(sa[:, ds(b * S, S)], pj[:, 1, :], ACT.Identity, bias=bo[:, 0:1]).then_inc(f_s.sem, 1)

            to_x(0)
            with act.Fori(0, NSEQ - 1) as b:
                f_body(b, False)
            f_body(NSEQ - 1, True)

            act.wait_ge(layers_zero, 1)
            with act.Fori(0, DEPTH) as l:
                def job(b, kind, j):
                    if kind == "proj":
                        act.wait_ge(proj_ready.sem, proj_ready.at(l, b, j))
                        act.wait_ge(n2_ready.sem, n2_ready.at(l, b, j - 1))
                        nc.scalar.activation(sq[:, :], pj[:, :, :].rearrange("p a b -> p (a b)"),
                                             ACT.Square).then_inc(sq_ready.sem, 1)
                    elif kind == "turn":
                        act.wait_ge(turn_ready.sem, turn_ready.at(l, b, j))
                        at = 128 * (j // 2)
                        src = pj[:, :, :].rearrange("p a (i c) -> p (a i) c", c=128)
                        if j % 2:
                            nc.scalar.copy(kT[0:64, :, 0, W + at:W + at + 128], src[0:64, :, :])
                            done = nc.scalar.copy(kT[64:128, :, 1, W + at:W + at + 128], src[64:128, :, :])
                        else:
                            done = nc.scalar.copy(qT[:, :, at:at + 128], src)
                        done.then_inc(turn_out.sem, 1)
                    elif kind == "v":
                        act.wait_ge(v_ready.sem, v_ready.at(l, b, j))
                        nk = tile_keys(j)
                        nc.scalar.copy(v[0:nk, j, :], pj[0:nk, :, :].rearrange("p a b -> p (a b)")
                                       ).then_inc(v_out.sem, 1)

                def exps(b, n):
                    t = n // 4
                    mq, nk = tile_queries(t), tile_keys(t)
                    act.wait_ge(mx_ready.sem, mx_ready.at(l, b, n))
                    act.wait_ge(tp_ready.sem, tp_ready.at(l, b, n - RING))
                    for i in range(4):
                        done = nc.scalar.activation(p[0:mq, n % RING, i * nk:(i + 1) * nk],
                                                    sc[0:mq, n % 2, i * nk:(i + 1) * nk], ACT.Exp,
                                                    bias=nmax[0:mq, n % RING, i:i + 1],
                                                    accum_out=psums[0:mq, n % RING, i:i + 1])
                    done.then_inc(p_ready.sem, 1)

                def half_out(b, m):
                    mm_ = m % (2 * NT)
                    t, half = mm_ // 2, mm_ % 2
                    mq = tile_queries(t)
                    act.wait_ge(pv_ready.sem, pv_ready.at(l, b, 2 * m + 1))
                    if m == 0:
                        act.wait_ge(y_ready.sem, y_ready.at(l, b, -1))
                    nc.scalar.copy(oT[:, 4 * half:4 * half + 4, QT * t:QT * t + mq],
                                   ob[:, half, 0:4 * mq].rearrange("p (i c) -> p i c", i=4)).then_inc(ot_out.sem, 1)

                def body(b, mode):
                    for slot in slots(mode):
                        if alive(slot, mode):
                            exps(b, slot)
                        if slot % 2 == HALF_LAG % 2 and alive(slot - HALF_LAG, mode):
                            half_out(b, (slot - HALF_LAG) // 2)
                        for kind, j, ahead, _ in jobs_at(slot, mode):
                            job(b + ahead, kind, j)

                body(-1, "prologue")
                body(0, "first")
                with act.Fori(1, NSEQ - 1) as b:
                    body(b, "mid")
                body(NSEQ - 1, "last")

                def gelus(b):
                    for c in range(3):
                        rows = CHUNK[c]
                        act.wait_ge(up_ready.sem, up_ready.at(l, b, 2 * c))
                        act.wait_ge(hid_ready.sem, hid_ready.at(l, b, c - 3))
                        nc.scalar.activation(gate[0:rows, c, :], up_bank[2 * c][0:rows, :], ACT.Gelu,
                                             bias=wffn[0:rows, VEC_AT + 6 + c:VEC_AT + 7 + c]).then_inc(gate_ready.sem, 1)

                act.wait_ge(wffn_in_s, (l + 1) * 16)
                with act.Fori(0, NSEQ - 1) as b:
                    gelus(b)
                gelus(NSEQ - 1)

            for b in range(NSEQ):
                act.wait_ge(x_ffn.sem, x_ffn.at(DEPTH - 1, b, 0))
                nc.scalar.activation(x[:, b * S:(b + 1) * S], x[:, b * S:(b + 1) * S], ACT.Silu).then_inc(e_g, 1)

        @block.vector
        def _(dve):
            for t in (f_ri, f_pt, n2_ready, rs_step, rot_ready, pt_ready, ri_ready,
                      x_attn, xc_ready, xn_ready, hid_ready, x_ffn):
                dve.sem_inc(t.sem, t.head_start)

            def shifted(dst, src_at):
                nc.vector.tensor_copy(dst[0:64, 0:S], x[0:64, ds(src_at, S)])
                return nc.vector.tensor_copy(dst[64:128, 1:S], x[64:128, ds(src_at, S - 1)])

            def rsqrt(link, y, n, tmp):
                i32 = mybir.dt.int32
                link(nc.vector.tensor_scalar(tmp.bitcast(i32), n.bitcast(i32), 1, None, ALU.logical_shift_right))
                link(nc.vector.tensor_scalar(y.bitcast(i32), tmp.bitcast(i32), -1.0, MAGIC, ALU.mult, ALU.add))
                for _ in range(NEWTON):
                    link(nc.vector.scalar_tensor_tensor(out=tmp, in0=y, scalar=-0.5, in1=y, op0=ALU.mult, op1=ALU.mult))
                    link(nc.vector.tensor_tensor(tmp, tmp, n, ALU.mult))
                    link(nc.vector.scalar_tensor_tensor(out=y, in0=tmp, scalar=1.5, in1=y, op0=ALU.add, op1=ALU.mult))

            dve.wait_ge(zero_ready, NZERO)
            dve.wait_ge(x_loaded, 16)

            def input_norm(b, piece):
                step = (0, 3, 5, 6 + RSQRT_STEPS)[piece]

                def link(ins):
                    nonlocal step
                    ins.then_inc(f_ln.sem, 1)
                    dve.wait_ge(f_ln.sem, f_ln.at(0, b, step))
                    step += 1

                xt = xtok[:, ds(b * S, S)].rearrange("p (t c) -> p t c", t=TT)
                wide = lambda a: a.unsqueeze(2).broadcast_to([128, TT, D])
                if piece == 0:
                    link(nc.vector.reduce_sum(st[:, 0, :], xt, AX.X))
                    link(nc.vector.tensor_scalar(st[:, 1, :], st[:, 0, :], 1.0 / D, None, ALU.mult))
                    link(nc.vector.tensor_tensor(xtc, xt, wide(st[:, 1, :]), ALU.subtract))
                elif piece == 1:
                    link(nc.vector.tensor_tensor(xtq, xtc, xtc, ALU.mult))
                    link(nc.vector.reduce_sum(st[:, 2, :], xtq, AX.X))
                elif piece == 2:
                    link(nc.vector.tensor_scalar(st[:, 3, :], st[:, 2, :], 1.0 / D, EPS, ALU.mult, ALU.add))
                    rsqrt(link, st[:, 4, :], st[:, 3, :], st[:, 5, :])
                else:
                    dve.wait_ge(f_xt.sem, f_xt.at(0, b, -1))
                    nc.vector.tensor_tensor(xtn, xtc, wide(st[:, 4, :]), ALU.mult).then_inc(f_xn.sem, 1)

            def f_body(b, last):
                for n in range(4):
                    dve.wait_ge(f_pj.sem, f_pj.at(0, b, 4 + n))
                    for r in range(2, 4):
                        done = nc.vector.tensor_copy(k1[32 * r:32 * r + 32, 4 * n + r, :], pj[32 * r:32 * r + 32, n % 2, :])
                    done.then_inc(f_pk.sem, 1)

                for slot in range(F + COPY_LAG):
                    if slot < F:
                        u = slot
                        nk = 128 * (u // H + 1)
                        dve.wait_ge(f_sc.sem, f_sc.at(0, b, u))
                        dve.wait_ge(f_p.sem, f_p.at(0, b, u - RING))
                        nc.vector.reduce_max(nmax[:, u % RING, 0:1], sc[:, u % 2, 0:nk], AX.X, negate=True).then_inc(f_mx.sem, 1)
                    if 1 <= slot <= F:
                        u = slot - 1
                        dve.wait_ge(f_p.sem, f_p.at(0, b, u))
                        nc.vector.reciprocal(rinv[:, u % RING, 0:1], psums[:, u % RING, 0:1]).then_inc(f_ri.sem, 1)
                    if slot >= COPY_LAG:
                        u = slot - COPY_LAG
                        nk = 128 * (u // H + 1)
                        dve.wait_ge(f_tp.sem, f_tp.at(0, b, u))
                        if u % 4 == 0:
                            dve.wait_ge(f_pv.sem, f_pv.at(0, b, u // 4 - 2))
                        nc.vector.tensor_copy(pT1[:, u % 8, 0:nk], tp[:, u % 2, 0:nk]).then_inc(f_pt.sem, 1)
                    if slot in NORM_SLOTS and not last:
                        input_norm(b + 1, NORM_SLOTS.index(slot))

            for piece in range(4):
                input_norm(0, piece)
            with dve.Fori(0, NSEQ - 1) as b:
                f_body(b, False)
            f_body(NSEQ - 1, True)

            dve.wait_ge(f_s.sem, f_s.at(0, NSEQ - 1, 0))
            dve.wait_ge(table_in_s, 16)
            with dve.Fori(0, DEPTH) as l:
                dve.wait_ge(wattn_in_s, (l + 1) * 16)
                nc.vector.tensor_tensor(ltable[:, :, :, :], table[:, :, :, :],
                                        wattn[:, SCALE_AT:WCOLS].rearrange("p (k d) -> p k d", k=4)
                                        .unsqueeze(2).broadcast_to([128, 4, TT, DH]), ALU.mult).then_inc(lt_ready.sem, 1)
                dve.wait_ge(lt_ready.sem, l + 1)

                def load_xs(b, first):
                    dve.wait_ge(x_ffn.sem, x_ffn.at(l - 1, b, 0))
                    if not first:
                        dve.wait_ge(proj_ready.sem, proj_ready.at(l, b, -1))
                        dve.wait_ge(v_ready.sem, v_ready.at(l, b, -1))
                    shifted(xs[:, W:W + S], b * S).then_inc(xs_ready.sem, 1)

                def products(b, j):
                    tau, kind = j // 2, j % 2
                    dve.wait_ge(sq_ready.sem, sq_ready.at(l, b, j))
                    dve.wait_ge(turn_ready.sem, turn_ready.at(l, b, j - 2))
                    dve.wait_ge(sum_ready.sem, sum_ready.at(l, b, j - 1))
                    src = pj[:, :, :].rearrange("p a (h d) -> p (a h) d", d=DH)
                    a3 = rot[:, kind, :].rearrange("p (h d) -> p h d", d=DH)
                    b3 = rot_s[:, :].rearrange("p (h d) -> p h d", d=DH)
                    tab = lambda k, lo, hi: (ltable[:, k, tau, lo:hi].unsqueeze(1)
                                             .broadcast_to([128, H, hi - lo]))
                    nc.vector.tensor_tensor(a3, src, tab(2 * kind, 0, DH), ALU.mult)
                    hd = DH // 2
                    nc.vector.tensor_tensor(b3[:, :, 0:hd], src[:, :, hd:DH], tab(2 * kind + 1, 0, hd), ALU.mult)
                    nc.vector.tensor_tensor(b3[:, :, hd:DH], src[:, :, 0:hd], tab(2 * kind + 1, hd, DH),
                                            ALU.mult).then_inc(rot_ready.sem, 1)

                def norms(b, j):
                    if j % 2 == 0:
                        dve.wait_ge(rs_step.sem, rs_step.at(l, b, j // 2 * RSQRT_STEPS - 1))
                    nc.vector.reduce_sum(n2[:, j % 2, :], sq[:, :].rearrange("p (h d) -> p h d", d=DH), AX.X
                                         ).then_inc(n2_ready.sem, 1)
                    if j % 2 == 0:
                        return
                    step = j // 2 * RSQRT_STEPS

                    def link(ins):
                        nonlocal step
                        ins.then_inc(rs_step.sem, 1)
                        dve.wait_ge(rs_step.sem, rs_step.at(l, b, step))
                        step += 1

                    dve.wait_ge(n2_ready.sem, n2_ready.at(l, b, j))
                    nc.vector.tensor_scalar(n2[:, :, :], n2[:, :, :], 1e-24, None, ALU.max).then_inc(n2_max.sem, 1)
                    dve.wait_ge(n2_max.sem, n2_max.at(l, b, j // 2))
                    dve.wait_ge(r_ready.sem, r_ready.at(l, b, j - 2))
                    rsqrt(link, rn[:, :, :], n2[:, :, :], rtmp[:, :, :])

                def top(b, n):
                    mq, nk = tile_queries(n // 4), tile_keys(n // 4)
                    dve.wait_ge(sc_ready.sem, sc_ready.at(l, b, n))
                    dve.wait_ge(p_ready.sem, p_ready.at(l, b, n - RING))
                    nc.vector.reduce_max(nmax[0:mq, n % RING, :],
                                         sc[0:mq, n % 2, 0:4 * nk].rearrange("p (i k) -> p i k", i=4),
                                         AX.X, negate=True).then_inc(mx_ready.sem, 1)

                def invert(b, n):
                    mq = tile_queries(n % UNITS // 4)
                    dve.wait_ge(p_ready.sem, p_ready.at(l, b, n))
                    nc.vector.reciprocal(rinv[0:mq, n % RING, :], psums[0:mq, n % RING, :]).then_inc(ri_ready.sem, 1)

                def copy_pt(b, n):
                    t = n % UNITS // 4
                    mq, nk = tile_queries(t), tile_keys(t)
                    dve.wait_ge(tp_ready.sem, tp_ready.at(l, b, n))
                    dve.wait_ge(pv_ready.sem, pv_ready.at(l, b, n - 2))
                    nc.vector.tensor_copy(pT[0:nk, n % 2, 0:4 * mq], tp[0:nk, n % 2, 0:4 * mq]).then_inc(pt_ready.sem, 1)

                def add_attention(b):
                    dve.wait_ge(y_ready.sem, y_ready.at(l, b, 0))
                    nc.vector.tensor_tensor(x[:, ds(b * S, S)], pj[:, 0, :], x[:, ds(b * S, S)],
                                            ALU.add).then_inc(x_attn.sem, 1)

                def body(b, mode):
                    for slot in slots(mode):
                        if slot == PROJ_SLOT[0] - 2 and mode != "last":
                            load_xs(b + 1, mode == "prologue")
                        if alive(slot, mode):
                            top(b, slot)
                        if alive(slot - 1, mode):
                            invert(b, slot - 1)
                        if alive(slot - COPY_LAG, mode):
                            copy_pt(b, slot - COPY_LAG)
                        for kind, j, ahead, _ in jobs_at(slot, mode):
                            if kind == "proj":
                                products(b + ahead, j)
                            elif kind == "norm":
                                norms(b + ahead, j)
                            elif kind == "out":
                                add_attention(b + ahead)

                body(-1, "prologue")
                body(0, "first")
                with dve.Fori(1, NSEQ - 1) as b:
                    body(b, "mid")
                body(NSEQ - 1, "last")

                def load_xm(b):
                    dve.wait_ge(x_attn.sem, x_attn.at(l, b, 0))
                    dve.wait_ge(mean_ready.sem, mean_ready.at(l, b, -1))
                    shifted(xm[:, :], b * S).then_inc(xm_ready.sem, 1)

                def centre(b):
                    dve.wait_ge(mean_ready.sem, mean_ready.at(l, b, 0))
                    nc.vector.tensor_tensor(xc[:, :], xm[:, :], tp[:, 0, :], ALU.subtract).then_inc(xc_ready.sem, 1)

                def norm(b):
                    step = 0

                    def link(ins):
                        nonlocal step
                        ins.then_inc(ln_step.sem, 1)
                        dve.wait_ge(ln_step.sem, ln_step.at(l, b, step))
                        step += 1

                    dve.wait_ge(var_ready.sem, var_ready.at(l, b, 0))
                    link(nc.vector.tensor_scalar(rstd[:, 0, :], tp[:, 0, 0:TT], EPS, None, ALU.add))
                    rsqrt(link, rstd[:, 1, :], rstd[:, 0, :], rstd[:, 2, :])
                    for t in range(TT):
                        done = nc.vector.tensor_scalar(diag[:, 128 * t:128 * t + 128], ident[:, :],
                                                       rstd[:, 1, t:t + 1], None, ALU.mult)
                    done.then_inc(rstd_ready.sem, 1)

                def scaled(b):
                    dve.wait_ge(wide_ready.sem, wide_ready.at(l, b, 0))
                    nc.vector.tensor_tensor(diag[:, :], xc[:, :], tp[:, 0, :], ALU.mult).then_inc(ln_step.sem, 1)
                    dve.wait_ge(ln_step.sem, ln_step.at(l, b, RSQRT_STEPS + 1))
                    nc.vector.tensor_scalar(xn[:, :], diag[:, :], wffn[:, VEC_AT:VEC_AT + 1],
                                            wffn[:, VEC_AT + 1:VEC_AT + 2], ALU.mult, ALU.add).then_inc(xn_ready.sem, 1)

                def hidden(b):
                    for c in range(3):
                        rows = CHUNK[c]
                        dve.wait_ge(up_ready.sem, up_ready.at(l, b, 2 * c + 1))
                        dve.wait_ge(gate_ready.sem, gate_ready.at(l, b, c))
                        dve.wait_ge(down_ready.sem, down_ready.at(l, b, -1))
                        nc.vector.scalar_tensor_tensor(out=hid[0:rows, c, :], in0=up_bank[2 * c + 1][0:rows, :],
                                                       scalar=wffn[0:rows, VEC_AT + 3 + c:VEC_AT + 4 + c],
                                                       in1=gate[0:rows, c, :], op0=ALU.add,
                                                       op1=ALU.mult).then_inc(hid_ready.sem, 1)

                def add_ffn(b):
                    dve.wait_ge(down_ready.sem, down_ready.at(l, b, 0))
                    nc.vector.scalar_tensor_tensor(out=x[:, ds(b * S, S)], in0=ob[:, 0, :],
                                                   scalar=wffn[:, VEC_AT + 2:VEC_AT + 3], in1=x[:, ds(b * S, S)],
                                                   op0=ALU.add, op1=ALU.add).then_inc(x_ffn.sem, 1)

                dve.wait_ge(wffn_in_s, (l + 1) * 16)
                load_xm(0)
                centre(0)
                norm(0)
                scaled(0)
                with dve.Fori(0, NSEQ - 1) as b:
                    load_xm(b + 1)
                    centre(b + 1)
                    hidden(b)
                    norm(b + 1)
                    scaled(b + 1)
                    add_ffn(b)
                hidden(NSEQ - 1)
                add_ffn(NSEQ - 1)

            dve.wait_ge(xtok_loaded, 16)
            for b in range(NSEQ + 1):
                if b < NSEQ:
                    dve.wait_ge(e_g, b + 1)
                    nc.vector.tensor_tensor(sa[:, b * S:(b + 1) * S], sa[:, b * S:(b + 1) * S],
                                            x[:, b * S:(b + 1) * S], ALU.mult).then_inc(e_r, 1)
                if b > 0:
                    dve.wait_ge(e_t, b)
                    nc.vector.tensor_tensor(qT[:, b - 1, :], tp[:, (b - 1) % 2, :],
                                            xtok[:, (b - 1) * S:b * S], ALU.add).then_inc(e_o, 1)

        @block.tensor
        def _(pe):
            pe.wait_ge(const_in, NCONST)
            pe.wait_ge(const_ready, 2)
            pe.wait_ge(zero_ready, NZERO)
            for t in (f_xt, f_tp, f_pv, f_y, turn_ready, tp_ready, pv_ready, y_ready, mean_ready, var_ready, down_ready):
                pe.sem_inc(t.sem, t.head_start)
            mm, tr = nc.tensor.matmul, nc.tensor.transpose

            def short_tile(t):
                if tile_queries(t) < QT:
                    pe.sem_inc(waits_past, 1)

            def turn_x(b):
                pe.wait_ge(f_xn.sem, f_xn.at(0, b, 0))
                for t in range(TT):
                    done = tr(pj[:, 0, 128 * t:128 * t + 128], xtn[:, t, :], ident[:, :])
                done.then_inc(f_xt.sem, 1)

            def f_body(b, last):
                pe.wait_ge(f_x.sem, f_x.at(0, b, 0))
                pe.wait_ge(f_s.sem, f_s.at(0, b, -1))
                for n in range(12):
                    pe.wait_ge(f_pe.sem, f_pe.at(0, b, n - 2))
                    if 6 <= n < 10:
                        pe.wait_ge(f_pk.sem, f_pk.at(0, b, n - 6))
                    if n < 8:
                        done = mm(pj[:, n % 2, :], wqk1[:, n, :], xb[:, :], start=True, stop=True)
                    else:
                        t = n - 8
                        done = mm(pj[:, n % 2, :], xb[:, 128 * t:128 * t + 128], wvo1[:, 0, :], start=True, stop=True)
                    done.then_inc(f_pj.sem, 1)
                pe.wait_ge(f_pe.sem, f_pe.at(0, b, 11))

                def scores(u):
                    t, jj, c = u // H, u % H // 4, u % 4
                    nk = 128 * (t + 1)
                    pe.wait_ge(f_p.sem, f_p.at(0, b, u - 2))
                    mm(sc[:, u % 2, 0:nk], qT1[:, jj, 128 * t:128 * t + 128], k1[:, 4 * jj + c, 0:nk],
                       start=True, stop=False)
                    mm(sc[:, u % 2, nk - 128:nk], ident_b[:, :], mask[:, 2, :],
                       start=False, stop=True).then_inc(f_sc.sem, 1)

                def turn_p(u):
                    pe.wait_ge(f_pn.sem, f_pn.at(0, b, u))
                    pe.wait_ge(f_pt.sem, f_pt.at(0, b, u - 2))
                    for k in range(u // H + 1):
                        done = tr(tp[:, u % 2, 128 * k:128 * k + 128], p[:, u % RING, 128 * k:128 * k + 128], ident[:, :])
                    done.then_inc(f_tp.sem, 1)

                def times_v(g):
                    t, jj = g // 4, g % 4
                    pe.wait_ge(f_pt.sem, f_pt.at(0, b, 4 * g + 3))
                    pe.wait_ge(f_oe.sem, f_oe.at(0, b, g - 2))
                    for k in range(t + 1):
                        for c in range(4):
                            h = 4 * c + jj
                            done = mm(ob[32 * c:32 * c + 32, g % 2, 0:128], v1[:, k, 32 * h:32 * h + 32],
                                      pT1[:, (4 * g + c) % 8, 128 * k:128 * k + 128], start=(k == 0), stop=(k == t))
                    done.then_inc(f_pv.sem, 1)

                for slot in range(F + 4):
                    if slot < F:
                        scores(slot)
                    if TURN_LAG <= slot < F + TURN_LAG:
                        turn_p(slot - TURN_LAG)
                    if slot >= 7 and slot % 4 == 3:
                        times_v((slot - 7) // 4)
                    if slot == XT_SLOT and not last:
                        turn_x(b + 1)
                pe.wait_ge(f_oe.sem, f_oe.at(0, b, G - 1))
                for jj in range(4):
                    done = mm(pj[:, 1, :], wvo1[:, 1, 128 * jj:128 * jj + 128], oT1[:, jj, :],
                              start=(jj == 0), stop=(jj == 3))
                done.then_inc(f_y.sem, 1)

            turn_x(0)
            with pe.Fori(0, NSEQ - 1) as b:
                f_body(b, False)
            f_body(NSEQ - 1, True)
            pe.wait_ge(f_s.sem, f_s.at(0, NSEQ - 1, 0))
            pe.wait_ge(layers_zero, 1)

            with pe.Fori(0, DEPTH) as l:
                pe.wait_ge(x_ffn.sem, x_ffn.at(l, 0, -1))
                pe.wait_ge(wattn_in_s, (l + 1) * 16)

                def job(b, kind, j, prev):
                    if kind in ("norm", "late"):
                        return
                    if prev:
                        k, n, ahead = prev
                        if k == "proj":
                            pe.wait_ge(rot_ready.sem, rot_ready.at(l, b - ahead, n))
                        elif k == "turn":
                            pe.wait_ge(turn_out.sem, turn_out.at(l, b - ahead, n))
                        elif k == "v":
                            pe.wait_ge(v_out.sem, v_out.at(l, b - ahead, n))
                        else:
                            pe.wait_ge(x_attn.sem, x_attn.at(l, b - ahead, n))
                    if kind == "proj":
                        if j == 0:
                            pe.wait_ge(xs_ready.sem, xs_ready.at(l, b, 0))
                        tau, base = j // 2, INNER * (j % 2)
                        for a in range(2):
                            done = mm(pj[:, a, :], xs[:, W + 128 * tau:W + 128 * tau + 128],
                                      wattn[:, base + 512 * a:base + 512 * a + 512], start=True, stop=True)
                        done.then_inc(proj_ready.sem, 1)
                    elif kind == "turn":
                        pe.wait_ge(r_ready.sem, r_ready.at(l, b, j))
                        for i in range(PAIRS):
                            done = tr(pj[:, i // 4, 128 * (i % 4):128 * (i % 4) + 128],
                                      rot[:, j % 2, 128 * i:128 * i + 128], ident[:, :])
                        done.then_inc(turn_ready.sem, 1)
                    elif kind == "v":
                        nk = tile_keys(j)
                        for a in range(2):
                            done = mm(pj[0:nk, a, :], xs[:, QT * j:QT * j + nk],
                                      wattn[:, 2 * INNER + 512 * a:2 * INNER + 512 * a + 512], start=True, stop=True)
                        done.then_inc(v_ready.sem, 1)
                    else:
                        pe.wait_ge(ot_out.sem, ot_out.at(l, b, 2 * NT - 1))
                        for i in range(PAIRS):
                            done = mm(pj[:, 0, :], wattn[:, 3 * INNER + D * i:3 * INNER + D * (i + 1)], oT[:, i, :],
                                      start=(i == 0), stop=(i == PAIRS - 1))
                        done.then_inc(y_ready.sem, 1)

                def scores(b, n):
                    t, quarter = n // 4, n % 4
                    mq, nk = tile_queries(t), tile_keys(t)
                    pe.wait_ge(p_ready.sem, p_ready.at(l, b, n - 2))
                    if n % 4 == 0:
                        pe.wait_ge(turn_out.sem, turn_out.at(l, b, 2 * ((QT * t + mq - 1) // 128) + 1))
                    for i in range(2):
                        pair = 2 * quarter + i
                        mm(sc[0:mq, n % 2, 2 * i * nk:2 * (i + 1) * nk], qT[:, pair, QT * t:QT * t + mq],
                           kT[:, pair, :, QT * t:QT * t + nk], start=(i == 0), stop=False)
                    mm(sc[0:mq, n % 2, 0:4 * nk], ident_b[0:mq, 0:mq],
                       mask[0:mq, 0 if t else 1, 0:nk].unsqueeze(1).broadcast_to([mq, 4, nk]),
                       start=False, stop=True).then_inc(sc_ready.sem, 1)

                def turn_p(b, n):
                    t = n % UNITS // 4
                    mq, nk = tile_queries(t), tile_keys(t)
                    pe.wait_ge(pn_ready.sem, pn_ready.at(l, b, n))
                    pe.wait_ge(pt_ready.sem, pt_ready.at(l, b, n - 2))
                    short_tile(t)
                    for i in range(4):
                        done = tr(tp[0:nk, n % 2, i * mq:(i + 1) * mq], p[0:mq, n % RING, i * nk:(i + 1) * nk],
                                  ident[0:mq, 0:mq])
                    done.then_inc(tp_ready.sem, 1)

                def times_v(b, n):
                    nn = n % UNITS
                    t, quarter = nn // 4, nn % 4
                    half = quarter // 2
                    mq, nk = tile_queries(t), tile_keys(t)
                    pe.wait_ge(pt_ready.sem, pt_ready.at(l, b, n))
                    if n % 2 == 0:
                        pe.wait_ge(ot_out.sem, ot_out.at(l, b, n // 2 - 2))
                    if nn % 4 == 0:
                        pe.wait_ge(v_out.sem, v_out.at(l, b, n // 4 if n >= 0 else n // 4))
                    short_tile(t)
                    for i in range(4):
                        h = 4 * quarter + i
                        par, at = i % 2, (2 * (quarter % 2) + i // 2) * mq
                        done = mm(ob[64 * par:64 * par + 64, half, at:at + mq], v[0:nk, t, h * DH:(h + 1) * DH],
                                  pT[0:nk, n % 2, i * mq:(i + 1) * mq], start=True, stop=True)
                    done.then_inc(pv_ready.sem, 1)

                def body(b, mode):
                    for slot in slots(mode):
                        if alive(slot, mode):
                            scores(b, slot)
                        if alive(slot - TURN_LAG, mode):
                            turn_p(b, slot - TURN_LAG)
                        if alive(slot - PV_LAG, mode):
                            times_v(b, slot - PV_LAG)
                        for kind, j, ahead, prev in jobs_at(slot, mode):
                            job(b + ahead, kind, j, prev)

                body(-1, "prologue")
                body(0, "first")
                with pe.Fori(1, NSEQ - 1) as b:
                    body(b, "mid")
                body(NSEQ - 1, "last")

                def mean(b):
                    pe.wait_ge(xm_ready.sem, xm_ready.at(l, b, 0))
                    pe.wait_ge(xn_ready.sem, xn_ready.at(l, b, -1))
                    mm(tp[:, 0, :], mean_w[:, :], xm[:, :], start=True, stop=True).then_inc(mean_ready.sem, 1)

                def variance(b):
                    pe.wait_ge(xc2_ready.sem, xc2_ready.at(l, b, 0))
                    for t in range(TT):
                        done = mm(tp[:, 0, t:t + 1], xc2[:, 128 * t:128 * t + 128], mean_w[:, 0:1], start=True, stop=True)
                    done.then_inc(var_ready.sem, 1)

                def widen(b):
                    pe.wait_ge(rstd_ready.sem, rstd_ready.at(l, b, 0))
                    mm(tp[:, 0, :], ones[:, :], diag[:, :], start=True, stop=True).then_inc(wide_ready.sem, 1)

                def up(b):
                    pe.wait_ge(xn_ready.sem, xn_ready.at(l, b, 0))
                    for c in range(3):
                        rows = CHUNK[c]
                        for side, used in ((0, gate_ready), (1, hid_ready)):
                            pe.wait_ge(used.sem, used.at(l, b, c - 3))
                            at = FC * c + (FF if side == 0 else 0)
                            mm(up_bank[2 * c + side][0:rows, :], wffn[:, at:at + rows], xn[:, :],
                               start=True, stop=True).then_inc(up_ready.sem, 1)

                def down(b):
                    pe.wait_ge(x_ffn.sem, x_ffn.at(l, b, -1))
                    for c in range(3):
                        rows = CHUNK[c]
                        pe.wait_ge(hid_ready.sem, hid_ready.at(l, b, c))
                        done = mm(ob[:, 0, :], wffn[0:rows, W2_AT + D * c:W2_AT + D * (c + 1)], hid[0:rows, c, :],
                                  start=(c == 0), stop=(c == 2))
                    done.then_inc(down_ready.sem, 1)

                pe.wait_ge(x_attn.sem, x_attn.at(l, NSEQ - 1, 0))
                pe.wait_ge(wffn_in_s, (l + 1) * 16)
                mean(0)
                variance(0)
                widen(0)
                with pe.Fori(0, NSEQ - 1) as b:
                    mean(b + 1)
                    up(b)
                    variance(b + 1)
                    down(b)
                    widen(b + 1)
                up(NSEQ - 1)
                down(NSEQ - 1)

            for b in range(NSEQ):
                pe.wait_ge(e_r, b + 1)
                if b >= 2:
                    pe.wait_ge(e_o, b - 1)
                for t in range(TT):
                    done = tr(tp[:, b % 2, 128 * t:128 * t + 128],
                              sa[:, b * S + 128 * t:b * S + 128 * t + 128], ident[:, :])
                done.then_inc(e_t, 1)


def rotary_constants():
    half = np.arange(0, DH, 2, dtype=np.float32)
    inv_freq = (np.float32(1.0) / np.power(np.float32(10000.0), half / np.float32(DH))).astype(np.float32)
    t = np.arange(S, dtype=np.float32)
    freqs = (t[:, None] * inv_freq[None, :]).astype(np.float32)
    base = ((half + np.float32(0.4 * DH)) / np.float32(1.4 * DH)).astype(np.float32)
    power = ((t - S // 2) / np.float32(W // 2)).astype(np.float32)
    scale = base.astype(np.float64)[None, :] ** power.astype(np.float64)[:, None]
    cos, sin = np.cos(freqs.astype(np.float64)), np.sin(freqs.astype(np.float64))
    both = lambda a, b: np.concatenate([a, b], -1)
    kinds = [both(cos * scale, cos * scale) * 8.0, both(-sin * scale, sin * scale) * 8.0,
             both(cos / scale, cos / scale), both(-sin / scale, sin / scale)]
    return np.ascontiguousarray(np.stack(kinds).reshape(4, TT, 128, DH).transpose(2, 0, 1, 3)).astype(np.float32)


def mask_constants():
    r, c = np.arange(128)[:, None], np.arange(128)[None, :]
    local = np.where((c >= r) & (c <= r + W), 0.0, NEG)
    start = np.where((c >= r) & (c <= r + W) & (c >= W), 0.0, NEG)
    causal = np.where(c <= r, 0.0, NEG)
    return np.ascontiguousarray(np.stack([local, start, causal], 1)).astype(np.float32)


def kernel(**inputs):
    import concourse.bacc as bacc
    from concourse.bass_utils import run_bass_kernel_spmd

    a = {k.replace("L0_", ""): np.asarray(v) for k, v in inputs.items()}
    f32 = np.float32
    wqk1 = np.zeros((128, 2, 4, 4, 32), f32)
    for n, name in enumerate(("attn_Wq", "attn_Wk")):
        wqk1[:, n, :, :, 0:CH] = a[name].reshape(D, 4, 4, CH).transpose(0, 2, 1, 3)
    wv1, wo1 = np.zeros((128, H, 32), f32), np.zeros((4, 32, 4, 128), f32)
    wv1[:, :, 0:CH] = a["attn_Wv"].reshape(D, H, CH)
    wo1[:, 0:CH] = a["attn_Wo"].reshape(4, 4, CH, D).transpose(0, 2, 1, 3)
    qs, ks = a["ffn_q_scale"], a["ffn_k_scale"]
    swap = lambda s: np.concatenate([s[:, DH // 2:], s[:, :DH // 2]], -1)
    scales = np.broadcast_to(np.stack([qs, swap(qs), ks, swap(ks)], 1).reshape(DEPTH, 1, 4 * DH), (DEPTH, 128, 4 * DH))
    wattn = np.concatenate([a["ffn_Wqkv"], a["ffn_Wo"].reshape(DEPTH, PAIRS, 128, D).transpose(0, 2, 1, 3)
                            .reshape(DEPTH, 128, PAIRS * D), scales], -1)
    w2 = np.zeros((DEPTH, 128, 3, D), f32)
    b1 = np.zeros((DEPTH, 128, 2, 3), f32)
    for c in range(3):
        at, rows = FC * c, CHUNK[c]
        w2[:, 0:rows, c, :] = a["ffn_W2"][:, at:at + rows, :]
        b1[:, 0:rows, 0, c] = a["ffn_b1"][:, at:at + rows]
        b1[:, 0:rows, 1, c] = a["ffn_b1"][:, FF + at:FF + at + rows]
    wffn = np.concatenate([a["ffn_W1"], w2.reshape(DEPTH, 128, 3 * D), a["ffn_ln_g"][:, :, None],
                           a["ffn_ln_b"][:, :, None], a["ffn_b2"][:, :, None], b1.reshape(DEPTH, 128, 6)], -1)
    arrays = {
        "in_x": a["attn_x"].reshape(NSEQ * S, D),
        "in_table": rotary_constants(),
        "in_ident": np.eye(128, dtype=f32),
        "in_mask": mask_constants(),
        "in_wqk1": wqk1.reshape(128, 8, 128),
        "in_wvo1": np.stack([wv1.reshape(128, 512), wo1.reshape(128, 512)], 1),
        "in_bo": a["attn_bo"].reshape(D, 1),
        "in_wattn": wattn.reshape(DEPTH * 128, WCOLS),
        "in_wffn": wffn.reshape(DEPTH * 128, FCOLS),
    }
    arrays = {k: np.ascontiguousarray(v) for k, v in arrays.items()}
    nc = bacc.Bacc("TRN2", target_bir_lowering=False, num_devices=1)
    args = [nc.dram_tensor(k, v.shape, mybir.dt.float32, kind="ExternalInput").ap() for k, v in arrays.items()]
    args.append(nc.dram_tensor("out", (NSEQ * S, D), mybir.dt.float32, kind="ExternalOutput").ap())
    build(nc, *args)
    r = run_bass_kernel_spmd(nc, [arrays], core_ids=[0])
    return r.results[0]["out"].reshape(NSEQ, S, D)
```

```python
import numpy as np
import concourse.bass as bass
from concourse import mybir
from contextlib import ExitStack

NSEQ, S, D = 8, 512, 128
TT = S // 128
DEPTH = 6
H = 16
CH = D // H
DH, INNER = 64, 16 * 64
PAIRS = H // 2
W = 32
QT = 96
NT = -(-S // QT)
FF = int(D * 4 * 2 / 3)
FC = -(-FF // 3)
CHUNK = [min(FC, FF - FC * j) for j in range(3)]
EPS = 1e-5
NEG = -1.0e30
WCOLS = 3 * INNER + PAIRS * D + 4 * DH
FCOLS = 2 * FF + 3 * D + 3 + 6

UNITS = NT * 4
TURN_LAG, COPY_LAG, PV_LAG = 3, 3, 4
HALF_LAG = 6
RING = 4
TAIL = 8
QKJOBS = 2 * TT
PROJ_SLOT = [11 + 3 * j for j in range(QKJOBS)]
TURN_SLOT = [17 + 3 * j - (j % 2) for j in range(QKJOBS)]
V_SLOT = [12 + 3 * v for v in range(NT)]
OUT_SLOT = 2 * UNITS + 6
ORDER = ["turn", "proj", "rotate", "norm", "late", "v", "out"]
BANKED = ("turn", "proj", "v", "out")
JOBS = sorted([(s, ORDER.index("proj"), j) for j, s in enumerate(PROJ_SLOT)]
              + [(s, ORDER.index("rotate"), j) for j, s in enumerate(PROJ_SLOT)]
              + [(s + 1, ORDER.index("norm"), j) for j, s in enumerate(PROJ_SLOT)]
              + [(s + 2, ORDER.index("late"), j) for j, s in enumerate(PROJ_SLOT) if j % 2]
              + [(s, ORDER.index("turn"), j) for j, s in enumerate(TURN_SLOT)]
              + [(s, ORDER.index("v"), v) for v, s in enumerate(V_SLOT)]
              + [(OUT_SLOT, ORDER.index("out"), 0)])


def tile_queries(t):
    return min(QT, S - QT * t)


def tile_keys(t):
    return min(128, S - QT * t + W)


MODES = ("prologue", "first", "mid", "last")


def slots(mode):
    return range(UNITS + (TAIL if mode == "last" else 0))


def alive(n, mode):
    return mode != "prologue" and n < UNITS and (n >= 0 or mode != "first")


def planned(mode):
    out = []
    late = (ORDER.index("turn"),) if mode == "prologue" else ()
    for s, k, j in sorted(JOBS, key=lambda job: (job[0] % UNITS, job[1] in late, job[1])):
        ahead = 1 - s // UNITS
        if mode == "mid" or (mode == "prologue" and ahead == 1) or (mode == "first" and ahead >= 0) \
                or (mode == "last" and ahead <= 0):
            out.append((s % UNITS, ORDER[k], j, ahead))
    if mode == "last":
        out.append((OUT_SLOT - UNITS, "out", 0, 0))
    return out


def jobs_at(slot, mode):
    jobs = planned(mode)
    out = []
    for job in jobs:
        if job[0] != slot:
            continue
        prev = None
        uses = [j for j in jobs if j[1] in (BANKED if mode != "prologue" else job[1:2])]
        if job in uses and job[1] in BANKED:
            at = uses.index(job)
            if at > 0:
                _, k, n, ahead = uses[at - 1]
                prev = (k, n, job[3] - ahead)
            elif mode != "prologue":
                _, k, n, ahead = [u for u in planned("mid") if u[1] in (("proj",) if mode == "first" else BANKED)][-1]
                prev = (k, n, job[3] - (ahead - 1))
        out.append((*job[1:], prev))
    return out


NEWTON = 3
RSQRT_STEPS = 2 + 3 * NEWTON
MAGIC = float(0x5f3759df)


class Tally:

    def __init__(self, sem, per_seq, head_start=0):
        self.sem, self.per_seq, self.head_start = sem, per_seq, head_start

    def at(self, layer, seq, n):
        return layer * (NSEQ * self.per_seq) + seq * self.per_seq + (n + 1 + self.head_start)


def build(nc, x_in, table_in, ident_in, mask_in, wqk1_in, wvo1_in, bo_in, wattn_in, wffn_in, out):
    fp32, bf16 = mybir.dt.float32, mybir.dt.bfloat16
    ALU, ACT, AX = mybir.AluOpType, mybir.ActivationFunctionType, mybir.AxisListType
    ds = bass.ds

    with ExitStack() as ctx:
        def sb(name, shape, dt=fp32):
            return ctx.enter_context(nc.sbuf_tensor(name, shape, dt))

        def sem(name):
            return ctx.enter_context(nc.semaphore(name))

        def tally(name, per_seq, head_start=0):
            return Tally(sem(name), per_seq, head_start)

        x = sb("x", [128, NSEQ * S])
        sa = sb("sa", [128, NSEQ * S])
        wattn = sb("wattn", [128, WCOLS])
        wffn = sb("wffn", [128, FCOLS])
        bo = sb("bo", [128, 1])
        ident = sb("ident", [128, 128])
        ident_b = sb("ident_b", [128, 128], bf16)
        mask = sb("mask", [128, 3, 128], bf16)
        table = sb("table", [128, 4, TT, DH])
        ltable = sb("ltable", [128, 4, TT, DH])
        mean_w = sb("mean_w", [128, 128])
        xs = sb("xs", [128, W + S])
        qT = sb("qT", [128, PAIRS, S])
        kT = sb("kT", [128, PAIRS, 2, W + S])
        v = sb("v", [128, NT, INNER])
        oT = sb("oT", [128, PAIRS, S])
        sq = sb("sq", [128, H * DH])
        maskf = sq[:, 0:384].rearrange("p (k c) -> p k c", c=128)
        rot = sb("rot", [128, 2, H * DH])
        rot_s = sb("rot_s", [128, H * DH])
        xn = sq[:, :].rearrange("p (a b) -> p a b", b=S)
        n2 = sb("n2", [128, 2, H])
        rn = sb("rn", [128, 2, H])
        rtmp = sb("rtmp", [128, 2, H])
        p = sb("p", [128, RING, 512])
        pT = sb("pT", [128, 2, 4 * QT])
        nmax = sb("nmax", [128, RING, 4])
        psums = sb("psums", [128, RING, 4])
        rinv = sb("rinv", [128, RING, 4])
        xm = sb("xm", [128, S])
        xc = sb("xc", [128, S])
        xc2 = sb("xc2", [128, S])
        rstd = sb("rstd", [128, 3, TT])
        diag = sb("diag", [128, S])
        ones = sb("ones", [128, 128])
        gate = sb("gate", [128, 3, S])
        hid = sb("hid", [128, 3, S])
        st = sb("st", [128, 6, TT])

        xtok = v[:, 0:4, :].rearrange("p a b -> p (a b)")
        oT1 = v[:, 4:6, :].rearrange("p a (b s) -> p (a b) s", s=S)
        qT1 = qT[:, 0:4, :]
        v1 = qT[:, 4:8, :]
        k1 = kT[:, :, :, :].rearrange("p a b c -> p (a b c)")[:, 0:H * S].rearrange("p (h s) -> p h s", s=S)
        pT1 = oT
        xb = sb("xb", [128, S])
        wqk1 = gate[:, :, :].rearrange("p a b -> p (a b)")[:, 0:8 * 128].rearrange("p (a b) -> p a b", b=128)
        wvo1 = hid[:, 0:2, :]
        xtn = xc[:, :].rearrange("p (t c) -> p t c", t=TT)
        xtc = xc2[:, :].rearrange("p (t c) -> p t c", t=TT)
        xtq = diag[:, :].rearrange("p (t c) -> p t c", t=TT)

        pj = ctx.enter_context(nc.psum_tensor("pj", [128, 2, 512], fp32))
        sc = ctx.enter_context(nc.psum_tensor("sc", [128, 2, 512], fp32))
        tp = ctx.enter_context(nc.psum_tensor("tp", [128, 2, 512], fp32))
        ob = ctx.enter_context(nc.psum_tensor("ob", [128, 2, 512], fp32))

        const_in, table_in_s, x_loaded, xtok_loaded, stored = sem("const_in"), sem("table_loaded"), sem("x_loaded"), sem("xtok_loaded"), sem("stored")
        wattn_in_s, wffn_in_s = sem("wattn_loaded"), sem("wffn_loaded")
        waits_past = sem("waits_past")
        const_ready, zero_ready, layers_zero = sem("const_ready"), sem("zero_ready"), sem("layers_zero")
        F, G = TT * H, TT * 4
        f_ln = tally("f_ln", 6 + RSQRT_STEPS)
        f_xn = tally("f_xn", 1)
        f_xt = tally("f_xt", 1, 1)
        f_x = tally("f_x", 1)
        f_pj = tally("f_pj", 12)
        f_pe = tally("f_pe", 12, 2)
        f_pk = tally("f_pk", 4, 0)
        f_sc = tally("f_sc", F)
        f_mx = tally("f_mx", F)
        f_p = tally("f_p", F, RING)
        f_ri = tally("f_ri", F, RING)
        f_pn = tally("f_pn", F)
        f_tp = tally("f_tp", F, RING)
        f_pt = tally("f_pt", F, 2)
        f_pv = tally("f_pv", G, 2)
        f_oe = tally("f_oe", G, 2)
        f_y = tally("f_y", 1, 1)
        f_s = tally("f_s", 1, 1)
        lt_ready = tally("lt_ready", 1)
        xs_ready = tally("xs_ready", 1)
        proj_ready = tally("proj_ready", 2 * QKJOBS)
        sq_ready = tally("sq_ready", 2 * QKJOBS, 1)
        n2_ready = tally("n2_ready", QKJOBS, 1)
        n2_max = tally("n2_max", TT)
        rs_step = tally("rs_step", TT * RSQRT_STEPS, 1)
        rot_ready = tally("rot_ready", 2 * QKJOBS, 1)
        sum_ready = tally("sum_ready", QKJOBS, 1)
        r_ready = tally("r_ready", QKJOBS, 2)
        turn_ready = tally("turn_ready", 2 * QKJOBS, 4)
        turn_out = tally("turn_out", 2 * QKJOBS, 1)
        v_ready = tally("v_ready", 2 * NT)
        v_out = tally("v_out", 2 * NT, 1)
        sc_ready = tally("sc_ready", UNITS)
        mx_ready = tally("mx_ready", UNITS)
        p_ready = tally("p_ready", UNITS, RING)
        ri_ready = tally("ri_ready", UNITS, RING)
        pn_ready = tally("pn_ready", UNITS)
        tp_ready = tally("tp_ready", UNITS, RING)
        pt_ready = tally("pt_ready", UNITS, 2)
        pv_ready = tally("pv_ready", UNITS, 2)
        ot_out = tally("ot_out", 2 * NT, 2)
        y_ready = tally("y_ready", 2, 1)
        x_attn = tally("x_attn", 2, 1)
        xm_ready = tally("xm_ready", 1)
        mean_ready = tally("mean_ready", 1, 1)
        xc_ready = tally("xc_ready", 1, 1)
        xc2_ready = tally("xc2_ready", 1)
        var_ready = tally("var_ready", 1, 1)
        rstd_ready = tally("rstd_ready", 1)
        wide_ready = tally("wide_ready", 1)
        ln_step = tally("ln_step", 1 + RSQRT_STEPS + 1)
        xn_ready = tally("xn_ready", 1, 1)
        up_ready = tally("up_ready", 6)
        gate_ready = tally("gate_ready", 3, 3)
        hid_ready = tally("hid_ready", 3, 3)
        down_ready = tally("down_ready", 1, 1)
        x_ffn = tally("x_ffn", 1, NSEQ)
        e_g, e_r, e_t, e_o = sem("e_g"), sem("e_r"), sem("e_t"), sem("e_o")

        alone = {"proj": pj, "turn": tp, "v": ob}

        block = ctx.enter_context(nc.Block())
        up_bank = [sc[:, 0, :], pj[:, 0, :], sc[:, 1, :], pj[:, 1, :], tp[:, 1, :], ob[:, 1, :]]
        W2_AT, VEC_AT, SCALE_AT = 2 * FF, 2 * FF + 3 * D, 3 * INNER + PAIRS * D
        NZERO = 7
        PROJ1 = [(kind, j) for j in range(4) for kind in "qk"] + [("v", t) for t in range(TT)]
        XT_SLOT, NORM_SLOTS = 44, (12, 20, 28, 36)
        NCONST = 16 * 5

        @block.sync
        def _(sp):
            sp.dma_start(xtok.rearrange("p (n c) -> p n c", c=D),
                         x_in.rearrange("(n p) c -> p n c", p=128)).then_inc(x_loaded, 16)
            for dst, src in ((ident[:, :], ident_in), (maskf[:, :, :], mask_in), (wqk1, wqk1_in),
                             (wvo1, wvo1_in), (bo[:, :], bo_in)):
                sp.dma_start(dst, src).then_inc(const_in, 16)
            sp.dma_start(table[:, :, :, :], table_in).then_inc(table_in_s, 16)
            sp.dma_start(wattn[:, :], wattn_in[0:128, :]).then_inc(wattn_in_s, 16)
            sp.dma_start(wffn[:, :], wffn_in[0:128, :]).then_inc(wffn_in_s, 16)
            with sp.Fori(1, DEPTH) as l:
                sp.wait_ge(y_ready.sem, y_ready.at(l - 1, NSEQ - 1, 1))
                sp.dma_start(wattn[:, :], wattn_in[ds(l * 128, 128), :]).then_inc(wattn_in_s, 16)
                sp.wait_ge(x_ffn.sem, x_ffn.at(l - 1, NSEQ - 1, 0))
                sp.dma_start(wffn[:, :], wffn_in[ds(l * 128, 128), :]).then_inc(wffn_in_s, 16)
            sp.wait_ge(y_ready.sem, y_ready.at(DEPTH - 1, NSEQ - 1, 1))
            sp.dma_start(xtok.rearrange("p (n c) -> p n c", c=D),
                         x_in.rearrange("(n p) c -> p n c", p=128)).then_inc(xtok_loaded, 16)
            for b in range(NSEQ):
                sp.wait_ge(e_o, b + 1)
                sp.dma_start(out.rearrange("(n p) c -> p n c", p=128)[:, TT * b:TT * (b + 1), :],
                             qT[:, b, :].rearrange("p (t c) -> p t c", t=TT)).then_inc(stored, 16)
            sp.wait_ge(stored, 16 * NSEQ)

        @block.gpsimd
        def _(pool):
            nc.gpsimd.memset(xs[:, :], 0.0).then_inc(zero_ready, 1)
            nc.gpsimd.memset(xm[:, :], 0.0).then_inc(zero_ready, 1)
            nc.gpsimd.memset(p[:, :, :], 0.0).then_inc(zero_ready, 1)
            nc.gpsimd.memset(rinv[:, :, :], 1.0).then_inc(zero_ready, 1)
            nc.gpsimd.memset(mean_w[:, :], 1.0 / D).then_inc(zero_ready, 1)
            nc.gpsimd.memset(ones[:, :], 1.0).then_inc(zero_ready, 1)
            nc.gpsimd.memset(kT[:, :, :, :], 0.0).then_inc(zero_ready, 1)
            for t in (r_ready, sum_ready):
                pool.sem_inc(t.sem, t.head_start)
            pool.wait_ge(zero_ready, NZERO)

            with pool.Fori(0, NSEQ) as b:
                for u in range(F):
                    nk = 128 * (u // H + 1)
                    pool.wait_ge(f_ri.sem, f_ri.at(0, b, u))
                    nc.gpsimd.tensor_tensor(p[:, u % RING, 0:nk], p[:, u % RING, 0:nk],
                                            rinv[:, u % RING, 0:1].broadcast_to([128, nk]), ALU.mult).then_inc(f_pn.sem, 1)

            pool.wait_ge(f_s.sem, f_s.at(0, NSEQ - 1, 0))
            nc.gpsimd.memset(kT[:, :, :, :], 0.0).then_inc(layers_zero, 1)

            with pool.Fori(0, DEPTH) as l:
                def probabilities(b, n):
                    pool.wait_ge(ri_ready.sem, ri_ready.at(l, b, n))
                    nk = tile_keys(n % UNITS // 4)
                    p3 = p[:, n % RING, 0:4 * nk].rearrange("p (i k) -> p i k", i=4)
                    nc.gpsimd.tensor_tensor(p3, p3, rinv[:, n % RING, :].unsqueeze(2).broadcast_to([128, 4, nk]),
                                            ALU.mult).then_inc(pn_ready.sem, 1)

                def unit_norm(b, j):
                    pool.wait_ge(sum_ready.sem, sum_ready.at(l, b, j))
                    pool.wait_ge(rs_step.sem, rs_step.at(l, b, (j // 2 + 1) * RSQRT_STEPS - 1))
                    r3 = rot[:, j % 2, :].rearrange("p (h d) -> p h d", d=DH)
                    nc.gpsimd.tensor_tensor(r3, r3, rn[:, j % 2, :].unsqueeze(2).broadcast_to([128, H, DH]),
                                            ALU.mult).then_inc(r_ready.sem, 1)

                def job(b, kind, j):
                    if kind == "rotate":
                        pool.wait_ge(rot_ready.sem, rot_ready.at(l, b, 2 * j + 1))
                        nc.gpsimd.tensor_tensor(rot[:, j % 2, :], rot[:, j % 2, :], rot_s[:, :],
                                                ALU.add).then_inc(sum_ready.sem, 1)
                    elif kind == "norm" and j % 2:
                        unit_norm(b, j - 1)
                    elif kind == "late":
                        unit_norm(b, j)

                def body(b, mode):
                    for slot in slots(mode):
                        n = slot - 1
                        if alive(n, mode):
                            probabilities(b, n)
                        for kind, j, ahead, _ in jobs_at(slot, mode):
                            job(b + ahead, kind, j)

                body(-1, "prologue")
                body(0, "first")
                with pool.Fori(1, NSEQ - 1) as b:
                    body(b, "mid")
                body(NSEQ - 1, "last")

                def square(b):
                    pool.wait_ge(xc_ready.sem, xc_ready.at(l, b, 0))
                    pool.wait_ge(var_ready.sem, var_ready.at(l, b, -1))
                    nc.gpsimd.tensor_tensor(xc2[:, :], xc[:, :], xc[:, :], ALU.mult).then_inc(xc2_ready.sem, 1)

                with pool.Fori(0, NSEQ) as b:
                    square(b)

        @block.scalar
        def _(act):
            act.wait_ge(const_in, NCONST)
            nc.scalar.copy(ident_b[:, :], ident[:, :]).then_inc(const_ready, 1)
            nc.scalar.copy(mask[:, :, :], maskf[:, :, :]).then_inc(const_ready, 1)
            for t in (f_pe, f_p, f_oe, f_s, sq_ready, turn_out, v_out, p_ready, ot_out, gate_ready):
                act.sem_inc(t.sem, t.head_start)
            act.wait_ge(zero_ready, NZERO)

            def to_x(b):
                act.wait_ge(f_xt.sem, f_xt.at(0, b, 0))
                nc.scalar.copy(x[:, ds(b * S, S)], pj[:, 0, :])
                nc.scalar.copy(xb[:, :], pj[:, 0, :]).then_inc(f_x.sem, 1)

            def f_body(b, last):
                def project_out(i):
                    act.wait_ge(f_pj.sem, f_pj.at(0, b, i))
                    kind, j = PROJ1[i]
                    src = pj[:, i % 2, :]
                    if kind == "q":
                        nc.scalar.mul(qT1[:, j, :], src, float(CH) ** -0.5).then_inc(f_pe.sem, 1)
                    elif kind == "k":
                        for r in range(2):
                            done = nc.scalar.copy(k1[32 * r:32 * r + 32, 4 * j + r, :], src[32 * r:32 * r + 32, :])
                        done.then_inc(f_pe.sem, 1)
                    else:
                        nc.scalar.copy(v1[:, j, :], src).then_inc(f_pe.sem, 1)

                project_out(0)
                project_out(1)

                def group_out(g):
                    act.wait_ge(f_pv.sem, f_pv.at(0, b, g))
                    if g == 0:
                        act.wait_ge(f_y.sem, f_y.at(0, b, -1))
                    t, jj = g // 4, g % 4
                    nc.scalar.copy(oT1[:, jj, 128 * t:128 * t + 128], ob[:, g % 2, 0:128]).then_inc(f_oe.sem, 1)

                for slot in range(F + 5):
                    if slot < F:
                        u = slot
                        nk = 128 * (u // H + 1)
                        act.wait_ge(f_mx.sem, f_mx.at(0, b, u))
                        act.wait_ge(f_tp.sem, f_tp.at(0, b, u - RING))
                        nc.scalar.activation(p[:, u % RING, 0:nk], sc[:, u % 2, 0:nk], ACT.Exp,
                                             bias=nmax[:, u % RING, 0:1],
                                             accum_out=psums[:, u % RING, 0:1]).then_inc(f_p.sem, 1)
                    if slot + 2 < len(PROJ1):
                        project_out(slot + 2)
                    if slot >= 8 and slot % 4 == 0:
                        group_out((slot - 8) // 4)
                    if slot == XT_SLOT + 1 and not last:
                        to_x(b + 1)
                act.wait_ge(f_y.sem, f_y.at(0, b, 0))
                nc.scalar.activation(sa[:, ds(b * S, S)], pj[:, 1, :], ACT.Identity, bias=bo[:, 0:1]).then_inc(f_s.sem, 1)

            to_x(0)
            with act.Fori(0, NSEQ - 1) as b:
                f_body(b, False)
            f_body(NSEQ - 1, True)

            act.wait_ge(layers_zero, 1)
            with act.Fori(0, DEPTH) as l:
                def job(b, kind, j, mode):
                    bank = alone[kind] if mode == "prologue" and kind in alone else pj
                    for a in range(2):
                        src = bank[:, a, :].rearrange("p (i c) -> p i c", c=128)
                        half = slice(4 * a, 4 * a + 4)
                        if kind == "proj":
                            act.wait_ge(proj_ready.sem, proj_ready.at(l, b, 2 * j + a))
                            if a == 0:
                                act.wait_ge(n2_ready.sem, n2_ready.at(l, b, j - 1))
                            nc.scalar.activation(sq[:, 512 * a:512 * a + 512], bank[:, a, :],
                                                 ACT.Square).then_inc(sq_ready.sem, 1)
                        elif kind == "turn":
                            act.wait_ge(turn_ready.sem, turn_ready.at(l, b, 2 * j + a))
                            at = 128 * (j // 2)
                            if j % 2:
                                nc.scalar.copy(kT[0:64, half, 0, W + at:W + at + 128], src[0:64, :, :])
                                done = nc.scalar.copy(kT[64:128, half, 1, W + at:W + at + 128], src[64:128, :, :])
                            else:
                                done = nc.scalar.copy(qT[:, half, at:at + 128], src)
                            done.then_inc(turn_out.sem, 1)
                        elif kind == "v":
                            act.wait_ge(v_ready.sem, v_ready.at(l, b, 2 * j + a))
                            nk = tile_keys(j)
                            nc.scalar.copy(v[0:nk, j, 512 * a:512 * a + 512], bank[0:nk, a, :]).then_inc(v_out.sem, 1)

                def exps(b, n):
                    t = n // 4
                    mq, nk = tile_queries(t), tile_keys(t)
                    act.wait_ge(mx_ready.sem, mx_ready.at(l, b, n))
                    act.wait_ge(tp_ready.sem, tp_ready.at(l, b, n - RING))
                    for i in range(4):
                        done = nc.scalar.activation(p[0:mq, n % RING, i * nk:(i + 1) * nk],
                                                    sc[0:mq, n % 2, i * nk:(i + 1) * nk], ACT.Exp,
                                                    bias=nmax[0:mq, n % RING, i:i + 1],
                                                    accum_out=psums[0:mq, n % RING, i:i + 1])
                    done.then_inc(p_ready.sem, 1)

                def half_out(b, m):
                    mm_ = m % (2 * NT)
                    t, half = mm_ // 2, mm_ % 2
                    mq = tile_queries(t)
                    act.wait_ge(pv_ready.sem, pv_ready.at(l, b, 2 * m + 1))
                    if m == 0:
                        act.wait_ge(y_ready.sem, y_ready.at(l, b, -1))
                    nc.scalar.copy(oT[:, 4 * half:4 * half + 4, QT * t:QT * t + mq],
                                   ob[:, half, 0:4 * mq].rearrange("p (i c) -> p i c", i=4)).then_inc(ot_out.sem, 1)

                def body(b, mode):
                    for slot in slots(mode):
                        if slot % 2 == HALF_LAG % 2 and alive(slot - HALF_LAG, mode):
                            half_out(b, (slot - HALF_LAG) // 2)
                        if alive(slot, mode):
                            exps(b, slot)
                        for kind, j, ahead, _ in jobs_at(slot, mode):
                            job(b + ahead, kind, j, mode)

                body(-1, "prologue")
                body(0, "first")
                with act.Fori(1, NSEQ - 1) as b:
                    body(b, "mid")
                body(NSEQ - 1, "last")

                def gelus(b):
                    for c in range(3):
                        rows = CHUNK[c]
                        act.wait_ge(up_ready.sem, up_ready.at(l, b, 2 * c))
                        act.wait_ge(hid_ready.sem, hid_ready.at(l, b, c - 3))
                        nc.scalar.activation(gate[0:rows, c, :], up_bank[2 * c][0:rows, :], ACT.Gelu,
                                             bias=wffn[0:rows, VEC_AT + 6 + c:VEC_AT + 7 + c]).then_inc(gate_ready.sem, 1)

                act.wait_ge(wffn_in_s, (l + 1) * 16)
                with act.Fori(0, NSEQ - 1) as b:
                    gelus(b)
                gelus(NSEQ - 1)

            for b in range(NSEQ):
                act.wait_ge(x_ffn.sem, x_ffn.at(DEPTH - 1, b, 0))
                nc.scalar.activation(x[:, b * S:(b + 1) * S], x[:, b * S:(b + 1) * S], ACT.Silu).then_inc(e_g, 1)

        @block.vector
        def _(dve):
            for t in (f_ri, f_pt, n2_ready, rs_step, rot_ready, pt_ready, ri_ready,
                      x_attn, xc_ready, xn_ready, hid_ready, x_ffn):
                dve.sem_inc(t.sem, t.head_start)

            def shifted(dst, src_at):
                nc.vector.tensor_copy(dst[0:64, 0:S], x[0:64, ds(src_at, S)])
                return nc.vector.tensor_copy(dst[64:128, 1:S], x[64:128, ds(src_at, S - 1)])

            def rsqrt(link, y, n, tmp):
                i32 = mybir.dt.int32
                link(nc.vector.tensor_scalar(tmp.bitcast(i32), n.bitcast(i32), 1, None, ALU.logical_shift_right))
                link(nc.vector.tensor_scalar(y.bitcast(i32), tmp.bitcast(i32), -1.0, MAGIC, ALU.mult, ALU.add))
                for _ in range(NEWTON):
                    link(nc.vector.scalar_tensor_tensor(out=tmp, in0=y, scalar=-0.5, in1=y, op0=ALU.mult, op1=ALU.mult))
                    link(nc.vector.tensor_tensor(tmp, tmp, n, ALU.mult))
                    link(nc.vector.scalar_tensor_tensor(out=y, in0=tmp, scalar=1.5, in1=y, op0=ALU.add, op1=ALU.mult))

            dve.wait_ge(zero_ready, NZERO)
            dve.wait_ge(x_loaded, 16)

            def input_norm(b, piece):
                step = (0, 3, 5, 6 + RSQRT_STEPS)[piece]

                def link(ins):
                    nonlocal step
                    ins.then_inc(f_ln.sem, 1)
                    dve.wait_ge(f_ln.sem, f_ln.at(0, b, step))
                    step += 1

                xt = xtok[:, ds(b * S, S)].rearrange("p (t c) -> p t c", t=TT)
                wide = lambda a: a.unsqueeze(2).broadcast_to([128, TT, D])
                if piece == 0:
                    link(nc.vector.reduce_sum(st[:, 0, :], xt, AX.X))
                    link(nc.vector.tensor_scalar(st[:, 1, :], st[:, 0, :], 1.0 / D, None, ALU.mult))
                    link(nc.vector.tensor_tensor(xtc, xt, wide(st[:, 1, :]), ALU.subtract))
                elif piece == 1:
                    link(nc.vector.tensor_tensor(xtq, xtc, xtc, ALU.mult))
                    link(nc.vector.reduce_sum(st[:, 2, :], xtq, AX.X))
                elif piece == 2:
                    link(nc.vector.tensor_scalar(st[:, 3, :], st[:, 2, :], 1.0 / D, EPS, ALU.mult, ALU.add))
                    rsqrt(link, st[:, 4, :], st[:, 3, :], st[:, 5, :])
                else:
                    dve.wait_ge(f_xt.sem, f_xt.at(0, b, -1))
                    nc.vector.tensor_tensor(xtn, xtc, wide(st[:, 4, :]), ALU.mult).then_inc(f_xn.sem, 1)

            def f_body(b, last):
                def project_out(i):
                    kind, j = PROJ1[i]
                    if kind != "k":
                        return
                    dve.wait_ge(f_pj.sem, f_pj.at(0, b, i))
                    for r in range(2, 4):
                        done = nc.vector.tensor_copy(k1[32 * r:32 * r + 32, 4 * j + r, :], pj[32 * r:32 * r + 32, i % 2, :])
                    done.then_inc(f_pk.sem, 1)

                project_out(1)
                for slot in range(F + COPY_LAG):
                    if slot < F:
                        u = slot
                        nk = 128 * (u // H + 1)
                        dve.wait_ge(f_sc.sem, f_sc.at(0, b, u))
                        dve.wait_ge(f_p.sem, f_p.at(0, b, u - RING))
                        nc.vector.reduce_max(nmax[:, u % RING, 0:1], sc[:, u % 2, 0:nk], AX.X, negate=True).then_inc(f_mx.sem, 1)
                    if 1 <= slot <= F:
                        u = slot - 1
                        dve.wait_ge(f_p.sem, f_p.at(0, b, u))
                        nc.vector.reciprocal(rinv[:, u % RING, 0:1], psums[:, u % RING, 0:1]).then_inc(f_ri.sem, 1)
                    if slot >= COPY_LAG:
                        u = slot - COPY_LAG
                        nk = 128 * (u // H + 1)
                        dve.wait_ge(f_tp.sem, f_tp.at(0, b, u))
                        if u % 4 == 0:
                            dve.wait_ge(f_pv.sem, f_pv.at(0, b, u // 4 - 2))
                        nc.vector.tensor_copy(pT1[:, u % 8, 0:nk], tp[:, u % 2, 0:nk]).then_inc(f_pt.sem, 1)
                    if slot + 2 < len(PROJ1):
                        project_out(slot + 2)
                    if slot in NORM_SLOTS and not last:
                        input_norm(b + 1, NORM_SLOTS.index(slot))

            for piece in range(4):
                input_norm(0, piece)
            with dve.Fori(0, NSEQ - 1) as b:
                f_body(b, False)
            f_body(NSEQ - 1, True)

            dve.wait_ge(f_s.sem, f_s.at(0, NSEQ - 1, 0))
            dve.wait_ge(table_in_s, 16)
            with dve.Fori(0, DEPTH) as l:
                dve.wait_ge(wattn_in_s, (l + 1) * 16)
                nc.vector.tensor_tensor(ltable[:, :, :, :], table[:, :, :, :],
                                        wattn[:, SCALE_AT:WCOLS].rearrange("p (k d) -> p k d", k=4)
                                        .unsqueeze(2).broadcast_to([128, 4, TT, DH]), ALU.mult).then_inc(lt_ready.sem, 1)
                dve.wait_ge(lt_ready.sem, l + 1)

                def load_xs(b, first):
                    dve.wait_ge(x_ffn.sem, x_ffn.at(l - 1, b, 0))
                    if not first:
                        dve.wait_ge(proj_ready.sem, proj_ready.at(l, b, -1))
                        dve.wait_ge(v_ready.sem, v_ready.at(l, b, -1))
                    shifted(xs[:, W:W + S], b * S).then_inc(xs_ready.sem, 1)

                def products(b, j):
                    tau, kind = j // 2, j % 2
                    for a in range(2):
                        dve.wait_ge(sq_ready.sem, sq_ready.at(l, b, 2 * j + a))
                        if a == 0:
                            dve.wait_ge(turn_ready.sem, turn_ready.at(l, b, 2 * (j - 2) + 1))
                            dve.wait_ge(sum_ready.sem, sum_ready.at(l, b, j - 1))
                        half = slice(512 * a, 512 * a + 512)
                        src = pj[:, a, :].rearrange("p (h d) -> p h d", d=DH)
                        a3 = rot[:, kind, half].rearrange("p (h d) -> p h d", d=DH)
                        b3 = rot_s[:, half].rearrange("p (h d) -> p h d", d=DH)
                        tab = lambda k, lo, hi: (ltable[:, k, tau, lo:hi].unsqueeze(1)
                                                 .broadcast_to([128, H // 2, hi - lo]))
                        nc.vector.tensor_tensor(a3, src, tab(2 * kind, 0, DH), ALU.mult)
                        hd = DH // 2
                        nc.vector.tensor_tensor(b3[:, :, 0:hd], src[:, :, hd:DH], tab(2 * kind + 1, 0, hd), ALU.mult)
                        nc.vector.tensor_tensor(b3[:, :, hd:DH], src[:, :, 0:hd], tab(2 * kind + 1, hd, DH),
                                                ALU.mult).then_inc(rot_ready.sem, 1)

                def norms(b, j):
                    if j % 2 == 0:
                        dve.wait_ge(rs_step.sem, rs_step.at(l, b, j // 2 * RSQRT_STEPS - 1))
                    nc.vector.reduce_sum(n2[:, j % 2, :], sq[:, :].rearrange("p (h d) -> p h d", d=DH), AX.X
                                         ).then_inc(n2_ready.sem, 1)
                    if j % 2 == 0:
                        return
                    step = j // 2 * RSQRT_STEPS

                    def link(ins):
                        nonlocal step
                        ins.then_inc(rs_step.sem, 1)
                        dve.wait_ge(rs_step.sem, rs_step.at(l, b, step))
                        step += 1

                    dve.wait_ge(n2_ready.sem, n2_ready.at(l, b, j))
                    nc.vector.tensor_scalar(n2[:, :, :], n2[:, :, :], 1e-24, None, ALU.max).then_inc(n2_max.sem, 1)
                    dve.wait_ge(n2_max.sem, n2_max.at(l, b, j // 2))
                    dve.wait_ge(r_ready.sem, r_ready.at(l, b, j - 2))
                    rsqrt(link, rn[:, :, :], n2[:, :, :], rtmp[:, :, :])

                def top(b, n):
                    mq, nk = tile_queries(n // 4), tile_keys(n // 4)
                    dve.wait_ge(sc_ready.sem, sc_ready.at(l, b, n))
                    dve.wait_ge(p_ready.sem, p_ready.at(l, b, n - RING))
                    nc.vector.reduce_max(nmax[0:mq, n % RING, :],
                                         sc[0:mq, n % 2, 0:4 * nk].rearrange("p (i k) -> p i k", i=4),
                                         AX.X, negate=True).then_inc(mx_ready.sem, 1)

                def invert(b, n):
                    mq = tile_queries(n % UNITS // 4)
                    dve.wait_ge(p_ready.sem, p_ready.at(l, b, n))
                    nc.vector.reciprocal(rinv[0:mq, n % RING, :], psums[0:mq, n % RING, :]).then_inc(ri_ready.sem, 1)

                def copy_pt(b, n):
                    t = n % UNITS // 4
                    mq, nk = tile_queries(t), tile_keys(t)
                    dve.wait_ge(tp_ready.sem, tp_ready.at(l, b, n))
                    dve.wait_ge(pv_ready.sem, pv_ready.at(l, b, n - 2))
                    nc.vector.tensor_copy(pT[0:nk, n % 2, 0:4 * mq], tp[0:nk, n % 2, 0:4 * mq]).then_inc(pt_ready.sem, 1)

                def add_attention(b):
                    for a in range(2):
                        dve.wait_ge(y_ready.sem, y_ready.at(l, b, a))
                        at = ds(b * S + a * (S // 2), S // 2)
                        nc.vector.tensor_tensor(x[:, at], pj[:, a, 0:S // 2], x[:, at], ALU.add).then_inc(x_attn.sem, 1)

                def body(b, mode):
                    for slot in slots(mode):
                        if slot == PROJ_SLOT[0] - 2 and mode != "last":
                            load_xs(b + 1, mode == "prologue")
                        if alive(slot, mode):
                            top(b, slot)
                        if alive(slot - 1, mode):
                            invert(b, slot - 1)
                        if alive(slot - COPY_LAG, mode):
                            copy_pt(b, slot - COPY_LAG)
                        for kind, j, ahead, _ in jobs_at(slot, mode):
                            if kind == "rotate":
                                products(b + ahead, j)
                            elif kind == "norm":
                                norms(b + ahead, j)
                            elif kind == "out":
                                add_attention(b + ahead)

                body(-1, "prologue")
                body(0, "first")
                with dve.Fori(1, NSEQ - 1) as b:
                    body(b, "mid")
                body(NSEQ - 1, "last")

                def load_xm(b):
                    dve.wait_ge(x_attn.sem, x_attn.at(l, b, 1))
                    dve.wait_ge(mean_ready.sem, mean_ready.at(l, b, -1))
                    dve.wait_ge(xc_ready.sem, xc_ready.at(l, b, -1))
                    shifted(xm[:, :], b * S).then_inc(xm_ready.sem, 1)

                def centre(b):
                    dve.wait_ge(mean_ready.sem, mean_ready.at(l, b, 0))
                    nc.vector.tensor_tensor(xc[:, :], xm[:, :], tp[:, 0, :], ALU.subtract).then_inc(xc_ready.sem, 1)

                def norm(b):
                    step = 0

                    def link(ins):
                        nonlocal step
                        ins.then_inc(ln_step.sem, 1)
                        dve.wait_ge(ln_step.sem, ln_step.at(l, b, step))
                        step += 1

                    dve.wait_ge(var_ready.sem, var_ready.at(l, b, 0))
                    link(nc.vector.tensor_scalar(rstd[:, 0, :], tp[:, 0, 0:TT], EPS, None, ALU.add))
                    rsqrt(link, rstd[:, 1, :], rstd[:, 0, :], rstd[:, 2, :])
                    for t in range(TT):
                        done = nc.vector.tensor_scalar(diag[:, 128 * t:128 * t + 128], ident[:, :],
                                                       rstd[:, 1, t:t + 1], None, ALU.mult)
                    done.then_inc(rstd_ready.sem, 1)

                def scaled(b, slot):
                    dve.wait_ge(wide_ready.sem, wide_ready.at(l, b, 0))
                    nc.vector.tensor_tensor(diag[:, :], xc[:, :], tp[:, 0, :], ALU.mult).then_inc(ln_step.sem, 1)
                    dve.wait_ge(ln_step.sem, ln_step.at(l, b, RSQRT_STEPS + 1))
                    nc.vector.tensor_scalar(xn[:, slot, :], diag[:, :], wffn[:, VEC_AT:VEC_AT + 1],
                                            wffn[:, VEC_AT + 1:VEC_AT + 2], ALU.mult, ALU.add).then_inc(xn_ready.sem, 1)

                def hidden(b, c):
                    rows = CHUNK[c]
                    dve.wait_ge(up_ready.sem, up_ready.at(l, b, 2 * c + 1))
                    dve.wait_ge(gate_ready.sem, gate_ready.at(l, b, c))
                    dve.wait_ge(down_ready.sem, down_ready.at(l, b, -1))
                    nc.vector.scalar_tensor_tensor(out=hid[0:rows, c, :], in0=up_bank[2 * c + 1][0:rows, :],
                                                   scalar=wffn[0:rows, VEC_AT + 3 + c:VEC_AT + 4 + c],
                                                   in1=gate[0:rows, c, :], op0=ALU.add,
                                                   op1=ALU.mult).then_inc(hid_ready.sem, 1)

                def add_ffn(b):
                    dve.wait_ge(down_ready.sem, down_ready.at(l, b, 0))
                    nc.vector.scalar_tensor_tensor(out=x[:, ds(b * S, S)], in0=ob[:, 0, :],
                                                   scalar=wffn[:, VEC_AT + 2:VEC_AT + 3], in1=x[:, ds(b * S, S)],
                                                   op0=ALU.add, op1=ALU.add).then_inc(x_ffn.sem, 1)

                dve.wait_ge(wffn_in_s, (l + 1) * 16)
                def step(b, parity, ahead):
                    if ahead >= 2:
                        load_xm(b + 2)
                    if ahead >= 1:
                        norm(b + 1)
                    hidden(b, 0)
                    hidden(b, 1)
                    if ahead >= 1:
                        scaled(b + 1, 1 - parity)
                    hidden(b, 2)
                    if ahead >= 2:
                        centre(b + 2)
                    add_ffn(b)

                load_xm(0)
                centre(0)
                norm(0)
                scaled(0, 0)
                load_xm(1)
                centre(1)
                with dve.Fori(0, NSEQ // 2 - 1) as i:
                    step(2 * i, 0, 2)
                    step(2 * i + 1, 1, 2)
                step(NSEQ - 2, 0, 1)
                step(NSEQ - 1, 1, 0)

            dve.wait_ge(xtok_loaded, 16)
            for b in range(NSEQ + 1):
                if b < NSEQ:
                    dve.wait_ge(e_g, b + 1)
                    nc.vector.tensor_tensor(sa[:, b * S:(b + 1) * S], sa[:, b * S:(b + 1) * S],
                                            x[:, b * S:(b + 1) * S], ALU.mult).then_inc(e_r, 1)
                if b > 0:
                    dve.wait_ge(e_t, b)
                    nc.vector.tensor_tensor(qT[:, b - 1, :], tp[:, (b - 1) % 2, :],
                                            xtok[:, (b - 1) * S:b * S], ALU.add).then_inc(e_o, 1)

        @block.tensor
        def _(pe):
            pe.wait_ge(const_in, NCONST)
            pe.wait_ge(const_ready, 2)
            pe.wait_ge(zero_ready, NZERO)
            for t in (f_xt, f_tp, f_pv, f_y, turn_ready, tp_ready, pv_ready, y_ready, mean_ready, var_ready, down_ready):
                pe.sem_inc(t.sem, t.head_start)
            mm, tr = nc.tensor.matmul, nc.tensor.transpose

            def short_tile(t):
                if tile_queries(t) < QT:
                    pe.sem_inc(waits_past, 1)

            def turn_x(b):
                pe.wait_ge(f_xn.sem, f_xn.at(0, b, 0))
                for t in range(TT):
                    done = tr(pj[:, 0, 128 * t:128 * t + 128], xtn[:, t, :], ident[:, :])
                done.then_inc(f_xt.sem, 1)

            def f_body(b, last):
                pe.wait_ge(f_x.sem, f_x.at(0, b, 0))
                pe.wait_ge(f_s.sem, f_s.at(0, b, -1))
                def project(i):
                    kind, j = PROJ1[i]
                    pe.wait_ge(f_pe.sem, f_pe.at(0, b, i - 2))
                    if i >= 2 and PROJ1[i - 2][0] == "k":
                        pe.wait_ge(f_pk.sem, f_pk.at(0, b, PROJ1[i - 2][1]))
                    if kind == "v":
                        done = mm(pj[:, i % 2, :], xb[:, 128 * j:128 * j + 128], wvo1[:, 0, :], start=True, stop=True)
                    else:
                        done = mm(pj[:, i % 2, :], wqk1[:, j + (4 if kind == "k" else 0), :], xb[:, :], start=True, stop=True)
                    done.then_inc(f_pj.sem, 1)

                project(0)
                project(1)

                def scores(u):
                    t, jj, c = u // H, u % H // 4, u % 4
                    nk = 128 * (t + 1)
                    if u < H and c == 0:
                        pe.wait_ge(f_pe.sem, f_pe.at(0, b, PROJ1.index(("k", jj))))
                        pe.wait_ge(f_pk.sem, f_pk.at(0, b, jj))
                    pe.wait_ge(f_p.sem, f_p.at(0, b, u - 2))
                    mm(sc[:, u % 2, 0:nk], qT1[:, jj, 128 * t:128 * t + 128], k1[:, 4 * jj + c, 0:nk],
                       start=True, stop=False)
                    mm(sc[:, u % 2, nk - 128:nk], ident_b[:, :], mask[:, 2, :],
                       start=False, stop=True).then_inc(f_sc.sem, 1)

                def turn_p(u):
                    pe.wait_ge(f_pn.sem, f_pn.at(0, b, u))
                    pe.wait_ge(f_pt.sem, f_pt.at(0, b, u - 2))
                    for k in range(u // H + 1):
                        done = tr(tp[:, u % 2, 128 * k:128 * k + 128], p[:, u % RING, 128 * k:128 * k + 128], ident[:, :])
                    done.then_inc(f_tp.sem, 1)

                def times_v(g):
                    t, jj = g // 4, g % 4
                    pe.wait_ge(f_pt.sem, f_pt.at(0, b, 4 * g + 3))
                    pe.wait_ge(f_oe.sem, f_oe.at(0, b, g - 2))
                    if jj == 0:
                        pe.wait_ge(f_pe.sem, f_pe.at(0, b, PROJ1.index(("v", t))))
                    for k in range(t + 1):
                        for c in range(4):
                            h = 4 * c + jj
                            done = mm(ob[32 * c:32 * c + 32, g % 2, 0:128], v1[:, k, 32 * h:32 * h + 32],
                                      pT1[:, (4 * g + c) % 8, 128 * k:128 * k + 128], start=(k == 0), stop=(k == t))
                    done.then_inc(f_pv.sem, 1)

                for slot in range(F + 4):
                    if slot < F:
                        scores(slot)
                    if TURN_LAG <= slot < F + TURN_LAG:
                        turn_p(slot - TURN_LAG)
                    if slot + 2 < len(PROJ1):
                        project(slot + 2)
                    if slot >= 7 and slot % 4 == 3:
                        times_v((slot - 7) // 4)
                    if slot == XT_SLOT and not last:
                        pe.wait_ge(f_pe.sem, f_pe.at(0, b, len(PROJ1) - 1))
                        turn_x(b + 1)
                pe.wait_ge(f_oe.sem, f_oe.at(0, b, G - 1))
                for jj in range(4):
                    done = mm(pj[:, 1, :], wvo1[:, 1, 128 * jj:128 * jj + 128], oT1[:, jj, :],
                              start=(jj == 0), stop=(jj == 3))
                done.then_inc(f_y.sem, 1)

            turn_x(0)
            with pe.Fori(0, NSEQ - 1) as b:
                f_body(b, False)
            f_body(NSEQ - 1, True)
            pe.wait_ge(f_s.sem, f_s.at(0, NSEQ - 1, 0))
            pe.wait_ge(layers_zero, 1)

            with pe.Fori(0, DEPTH) as l:
                pe.wait_ge(x_ffn.sem, x_ffn.at(l, 0, -1))
                pe.wait_ge(wattn_in_s, (l + 1) * 16)

                def job(b, kind, j, prev, mode):
                    if kind not in BANKED:
                        return
                    bank = alone[kind] if mode == "prologue" else pj
                    tau, nk = j // 2, tile_keys(j) if kind == "v" else 0
                    if kind == "proj" and j == 0:
                        pe.wait_ge(xs_ready.sem, xs_ready.at(l, b, 0))
                    elif kind == "turn":
                        pe.wait_ge(r_ready.sem, r_ready.at(l, b, j))
                    elif kind == "out":
                        pe.wait_ge(ot_out.sem, ot_out.at(l, b, 2 * NT - 1))
                    for a in range(2):
                        if prev:
                            k, n, ahead = prev
                            used = {"proj": rot_ready, "turn": turn_out, "v": v_out, "out": x_attn}[k]
                            pe.wait_ge(used.sem, used.at(l, b - ahead, 2 * n + a))
                        if kind == "proj":
                            at = INNER * (j % 2) + 512 * a
                            mm(bank[:, a, :], xs[:, W + 128 * tau:W + 128 * tau + 128], wattn[:, at:at + 512],
                               start=True, stop=True).then_inc(proj_ready.sem, 1)
                        elif kind == "turn":
                            for i in range(4 * a, 4 * a + 4):
                                done = tr(bank[:, a, 128 * (i % 4):128 * (i % 4) + 128],
                                          rot[:, j % 2, 128 * i:128 * i + 128], ident[:, :])
                            done.then_inc(turn_ready.sem, 1)
                        elif kind == "v":
                            at = 2 * INNER + 512 * a
                            mm(bank[0:nk, a, :], xs[:, QT * j:QT * j + nk], wattn[:, at:at + 512],
                               start=True, stop=True).then_inc(v_ready.sem, 1)
                        else:
                            for i in range(PAIRS):
                                done = mm(bank[:, a, 0:S // 2], wattn[:, 3 * INNER + D * i:3 * INNER + D * (i + 1)],
                                          oT[:, i, a * (S // 2):(a + 1) * (S // 2)], start=(i == 0), stop=(i == PAIRS - 1))
                            done.then_inc(y_ready.sem, 1)

                def scores(b, n):
                    t, quarter = n // 4, n % 4
                    mq, nk = tile_queries(t), tile_keys(t)
                    pe.wait_ge(p_ready.sem, p_ready.at(l, b, n - 2))
                    if n % 4 == 0:
                        pe.wait_ge(turn_out.sem, turn_out.at(l, b, 4 * ((QT * t + mq - 1) // 128) + 3))
                    for i in range(2):
                        pair = 2 * quarter + i
                        mm(sc[0:mq, n % 2, 2 * i * nk:2 * (i + 1) * nk], qT[:, pair, QT * t:QT * t + mq],
                           kT[:, pair, :, QT * t:QT * t + nk], start=(i == 0), stop=False)
                    mm(sc[0:mq, n % 2, 0:4 * nk], ident_b[0:mq, 0:mq],
                       mask[0:mq, 0 if t else 1, 0:nk].unsqueeze(1).broadcast_to([mq, 4, nk]),
                       start=False, stop=True).then_inc(sc_ready.sem, 1)

                def turn_p(b, n):
                    t = n % UNITS // 4
                    mq, nk = tile_queries(t), tile_keys(t)
                    pe.wait_ge(pn_ready.sem, pn_ready.at(l, b, n))
                    pe.wait_ge(pt_ready.sem, pt_ready.at(l, b, n - 2))
                    short_tile(t)
                    for i in range(4):
                        done = tr(tp[0:nk, n % 2, i * mq:(i + 1) * mq], p[0:mq, n % RING, i * nk:(i + 1) * nk],
                                  ident[0:mq, 0:mq])
                    done.then_inc(tp_ready.sem, 1)

                def times_v(b, n):
                    nn = n % UNITS
                    t, quarter = nn // 4, nn % 4
                    half = quarter // 2
                    mq, nk = tile_queries(t), tile_keys(t)
                    pe.wait_ge(pt_ready.sem, pt_ready.at(l, b, n))
                    if n % 2 == 0:
                        pe.wait_ge(ot_out.sem, ot_out.at(l, b, n // 2 - 2))
                    if nn % 4 == 0:
                        pe.wait_ge(v_out.sem, v_out.at(l, b, 2 * (n // 4) + 1))
                    short_tile(t)
                    for i in range(4):
                        h = 4 * quarter + i
                        par, at = i % 2, (2 * (quarter % 2) + i // 2) * mq
                        done = mm(ob[64 * par:64 * par + 64, half, at:at + mq], v[0:nk, t, h * DH:(h + 1) * DH],
                                  pT[0:nk, n % 2, i * mq:(i + 1) * mq], start=True, stop=True)
                    done.then_inc(pv_ready.sem, 1)

                def body(b, mode):
                    for slot in slots(mode):
                        if alive(slot, mode):
                            scores(b, slot)
                        if alive(slot - PV_LAG, mode):
                            times_v(b, slot - PV_LAG)
                        if alive(slot - TURN_LAG, mode):
                            turn_p(b, slot - TURN_LAG)
                        for kind, j, ahead, prev in jobs_at(slot, mode):
                            job(b + ahead, kind, j, prev, mode)

                body(-1, "prologue")
                done_before = planned("prologue")
                pe.wait_ge(turn_out.sem, turn_out.at(l, 0, 2 * max(j for _, k, j, _ in done_before if k == "turn") + 1))
                pe.wait_ge(v_out.sem, v_out.at(l, 0, 2 * max(j for _, k, j, _ in done_before if k == "v") + 1))
                body(0, "first")
                with pe.Fori(1, NSEQ - 1) as b:
                    body(b, "mid")
                body(NSEQ - 1, "last")

                def mean(b):
                    pe.wait_ge(xm_ready.sem, xm_ready.at(l, b, 0))
                    pe.wait_ge(xn_ready.sem, xn_ready.at(l, b, -1))
                    mm(tp[:, 0, :], mean_w[:, :], xm[:, :], start=True, stop=True).then_inc(mean_ready.sem, 1)

                def variance(b):
                    pe.wait_ge(xc2_ready.sem, xc2_ready.at(l, b, 0))
                    for t in range(TT):
                        done = mm(tp[:, 0, t:t + 1], xc2[:, 128 * t:128 * t + 128], mean_w[:, 0:1], start=True, stop=True)
                    done.then_inc(var_ready.sem, 1)

                def widen(b):
                    pe.wait_ge(rstd_ready.sem, rstd_ready.at(l, b, 0))
                    mm(tp[:, 0, :], ones[:, :], diag[:, :], start=True, stop=True).then_inc(wide_ready.sem, 1)

                def up(b, slot, c):
                    rows = CHUNK[c]
                    if c == 0:
                        pe.wait_ge(xn_ready.sem, xn_ready.at(l, b, 0))
                    for side, used in ((0, gate_ready), (1, hid_ready)):
                        pe.wait_ge(used.sem, used.at(l, b, c - 3))
                        at = FC * c + (FF if side == 0 else 0)
                        mm(up_bank[2 * c + side][0:rows, :], wffn[:, at:at + rows], xn[:, slot, :],
                           start=True, stop=True).then_inc(up_ready.sem, 1)

                def down(b):
                    pe.wait_ge(x_ffn.sem, x_ffn.at(l, b, -1))
                    for c in range(3):
                        rows = CHUNK[c]
                        pe.wait_ge(hid_ready.sem, hid_ready.at(l, b, c))
                        done = mm(ob[:, 0, :], wffn[0:rows, W2_AT + D * c:W2_AT + D * (c + 1)], hid[0:rows, c, :],
                                  start=(c == 0), stop=(c == 2))
                    done.then_inc(down_ready.sem, 1)

                pe.wait_ge(x_attn.sem, x_attn.at(l, NSEQ - 1, 1))
                pe.wait_ge(wffn_in_s, (l + 1) * 16)
                def step(b, parity, ahead):
                    up(b, parity, 0)
                    up(b, parity, 1)
                    if ahead >= 1:
                        widen(b + 1)
                    up(b, parity, 2)
                    if ahead >= 2:
                        mean(b + 2)
                    down(b)
                    if ahead >= 2:
                        variance(b + 2)

                mean(0)
                variance(0)
                widen(0)
                mean(1)
                variance(1)
                with pe.Fori(0, NSEQ // 2 - 1) as i:
                    step(2 * i, 0, 2)
                    step(2 * i + 1, 1, 2)
                step(NSEQ - 2, 0, 1)
                step(NSEQ - 1, 1, 0)

            for b in range(NSEQ):
                pe.wait_ge(e_r, b + 1)
                if b >= 2:
                    pe.wait_ge(e_o, b - 1)
                for t in range(TT):
                    done = tr(tp[:, b % 2, 128 * t:128 * t + 128],
                              sa[:, b * S + 128 * t:b * S + 128 * t + 128], ident[:, :])
                done.then_inc(e_t, 1)


def rotary_constants():
    half = np.arange(0, DH, 2, dtype=np.float32)
    inv_freq = (np.float32(1.0) / np.power(np.float32(10000.0), half / np.float32(DH))).astype(np.float32)
    t = np.arange(S, dtype=np.float32)
    freqs = (t[:, None] * inv_freq[None, :]).astype(np.float32)
    base = ((half + np.float32(0.4 * DH)) / np.float32(1.4 * DH)).astype(np.float32)
    power = ((t - S // 2) / np.float32(W // 2)).astype(np.float32)
    scale = base.astype(np.float64)[None, :] ** power.astype(np.float64)[:, None]
    cos, sin = np.cos(freqs.astype(np.float64)), np.sin(freqs.astype(np.float64))
    both = lambda a, b: np.concatenate([a, b], -1)
    kinds = [both(cos * scale, cos * scale) * 8.0, both(-sin * scale, sin * scale) * 8.0,
             both(cos / scale, cos / scale), both(-sin / scale, sin / scale)]
    return np.ascontiguousarray(np.stack(kinds).reshape(4, TT, 128, DH).transpose(2, 0, 1, 3)).astype(np.float32)


def mask_constants():
    r, c = np.arange(128)[:, None], np.arange(128)[None, :]
    local = np.where((c >= r) & (c <= r + W), 0.0, NEG)
    start = np.where((c >= r) & (c <= r + W) & (c >= W), 0.0, NEG)
    causal = np.where(c <= r, 0.0, NEG)
    return np.ascontiguousarray(np.stack([local, start, causal], 1)).astype(np.float32)


def kernel(**inputs):
    import concourse.bacc as bacc
    from concourse.bass_utils import run_bass_kernel_spmd

    a = {k.replace("L0_", ""): np.asarray(v) for k, v in inputs.items()}
    f32 = np.float32
    wqk1 = np.zeros((128, 2, 4, 4, 32), f32)
    for n, name in enumerate(("attn_Wq", "attn_Wk")):
        wqk1[:, n, :, :, 0:CH] = a[name].reshape(D, 4, 4, CH).transpose(0, 2, 1, 3)
    wv1, wo1 = np.zeros((128, H, 32), f32), np.zeros((4, 32, 4, 128), f32)
    wv1[:, :, 0:CH] = a["attn_Wv"].reshape(D, H, CH)
    wo1[:, 0:CH] = a["attn_Wo"].reshape(4, 4, CH, D).transpose(0, 2, 1, 3)
    qs, ks = a["ffn_q_scale"], a["ffn_k_scale"]
    swap = lambda s: np.concatenate([s[:, DH // 2:], s[:, :DH // 2]], -1)
    scales = np.broadcast_to(np.stack([qs, swap(qs), ks, swap(ks)], 1).reshape(DEPTH, 1, 4 * DH), (DEPTH, 128, 4 * DH))
    wattn = np.concatenate([a["ffn_Wqkv"], a["ffn_Wo"].reshape(DEPTH, PAIRS, 128, D).transpose(0, 2, 1, 3)
                            .reshape(DEPTH, 128, PAIRS * D), scales], -1)
    w2 = np.zeros((DEPTH, 128, 3, D), f32)
    b1 = np.zeros((DEPTH, 128, 2, 3), f32)
    for c in range(3):
        at, rows = FC * c, CHUNK[c]
        w2[:, 0:rows, c, :] = a["ffn_W2"][:, at:at + rows, :]
        b1[:, 0:rows, 0, c] = a["ffn_b1"][:, at:at + rows]
        b1[:, 0:rows, 1, c] = a["ffn_b1"][:, FF + at:FF + at + rows]
    wffn = np.concatenate([a["ffn_W1"], w2.reshape(DEPTH, 128, 3 * D), a["ffn_ln_g"][:, :, None],
                           a["ffn_ln_b"][:, :, None], a["ffn_b2"][:, :, None], b1.reshape(DEPTH, 128, 6)], -1)
    arrays = {
        "in_x": a["attn_x"].reshape(NSEQ * S, D),
        "in_table": rotary_constants(),
        "in_ident": np.eye(128, dtype=f32),
        "in_mask": mask_constants(),
        "in_wqk1": wqk1.reshape(128, 8, 128),
        "in_wvo1": np.stack([wv1.reshape(128, 512), wo1.reshape(128, 512)], 1),
        "in_bo": a["attn_bo"].reshape(D, 1),
        "in_wattn": wattn.reshape(DEPTH * 128, WCOLS),
        "in_wffn": wffn.reshape(DEPTH * 128, FCOLS),
    }
    arrays = {k: np.ascontiguousarray(v) for k, v in arrays.items()}
    nc = bacc.Bacc("TRN2", target_bir_lowering=False, num_devices=1)
    args = [nc.dram_tensor(k, v.shape, mybir.dt.float32, kind="ExternalInput").ap() for k, v in arrays.items()]
    args.append(nc.dram_tensor("out", (NSEQ * S, D), mybir.dt.float32, kind="ExternalOutput").ap())
    build(nc, *args)
    r = run_bass_kernel_spmd(nc, [arrays], core_ids=[0])
    return r.results[0]["out"].reshape(NSEQ, S, D)
```
